# Optimizing a Trainium2 kernel written in Bass

```python
import numpy as np
import jax
import jax.numpy as jnp

def _softmax(x, axis=-1):
    return jax.nn.softmax(x, axis=axis)

def _gelu(x):
    return jax.nn.gelu(x, approximate=True)

def _silu(x):
    return jax.nn.silu(x)

def _sigmoid(x):
    return jax.nn.sigmoid(x)

def _layernorm(x, axis=-1, eps=1e-05):
    m = jnp.mean(x, axis=axis, keepdims=True)
    v = jnp.var(x, axis=axis, keepdims=True)
    return (x - m) / jnp.sqrt(v + eps)

def _scatter_add(tgt, idx, src, axis=0):
    return tgt.at[idx].add(src)

def _segment_sum(src, seg, n):
    return jax.ops.segment_sum(src, seg, n)
kernel_name = 'mk_decoder_preln_d1_seqx_r8_9339b6'

def setup_inputs(seed: int=0):
    np.random.seed(seed)
    _w = jnp.asarray

    def _rec_inputs():
        import jax
        import jax.numpy as jnp
        _rk = jax.random.key(seed)
        x = -7.109e-05 + 0.9999 * jax.random.normal(jax.random.fold_in(_rk, 1), (16, 256, 128), jnp.float32)
        _lenS = 256 - jax.random.randint(jax.random.fold_in(_rk, 7), (16,), 0, max(1, 256 // 4) + 1, jnp.int32)
        _lenS2 = 1601 - jax.random.randint(jax.random.fold_in(_rk, 8), (16,), 0, max(1, 1601 // 4) + 1, jnp.int32)
        _ctx_768P = jax.random.normal(jax.random.fold_in(_rk, 11), (16, 16, 96), jnp.float32)
        _ctx_768c = jax.random.dirichlet(jax.random.fold_in(_rk, 511), 0.3 * jnp.ones((16,), jnp.float32), (16, 1601))
        _ctx_768t = jnp.einsum('bsk,bkd->bsd', _ctx_768c, _ctx_768P)
        _ctx_768t = _ctx_768t * jax.lax.rsqrt(jnp.mean(jnp.square(_ctx_768t)) + 1e-12) * 0.953939
        ctx_768 = 0.000486113 + 1.00014 * (_ctx_768t + 0.3 * jax.random.normal(jax.random.fold_in(_rk, 611), (16, 1601, 96), jnp.float32))
        return (x, ctx_768)
    x, ctx_768 = _rec_inputs()

    def _L0_attn_setup():
        import jax, jax.numpy as jnp
        import numpy as np
        EMBED_DIM = 128
        key = jax.random.key(seed)
        ks = jax.random.split(key, 9)
        B, S, D = (4, 512, EMBED_DIM)
        s = 1.0 / np.sqrt(D)
        inp = {'x': jax.random.normal(ks[0], (B, S, D), dtype=jnp.float32)}
        names = ['q', 'k', 'v', 'out']
        for i, n in enumerate(names):
            inp[f'w_{n}'] = jax.random.uniform(ks[1 + 2 * i], (D, D), jnp.float32, -s, s)
            inp[f'b_{n}'] = jax.random.uniform(ks[2 + 2 * i], (D,), jnp.float32, -s, s)
        return inp
    _L0_attn_all = _L0_attn_setup()
    _L0_attn_in = {k: v for k, v in _L0_attn_all.items() if k in ('w_q', 'b_q', 'w_k', 'b_k', 'w_v', 'b_v', 'w_out', 'b_out')}
    del _L0_attn_all

    def _L0_xattn_setup():
        import jax, jax.numpy as jnp
        import numpy as np
        HEADS = 16
        DIM_HEAD = 64
        SCALE = DIM_HEAD ** (-0.5)
        key = jax.random.key(seed)
        ks = jax.random.split(key, 7)
        B, Nq, Dq = (16, 512, 128)
        Nc, Dc = (77, 96)
        inner = HEADS * DIM_HEAD
        return {'x': jax.random.normal(ks[0], (B, Nq, Dq), jnp.float32), 'context': jax.random.normal(ks[1], (B, Nc, Dc), jnp.float32), 'Wq': jax.random.normal(ks[2], (Dq, inner), jnp.float32) * Dq ** (-0.5), 'Wk': jax.random.normal(ks[3], (Dc, inner), jnp.float32) * Dc ** (-0.5), 'Wv': jax.random.normal(ks[4], (Dc, inner), jnp.float32) * Dc ** (-0.5), 'Wo': jax.random.normal(ks[5], (inner, Dq), jnp.float32) * inner ** (-0.5), 'bo': jnp.zeros((Dq,), jnp.float32)}
    _L0_xattn_all = _L0_xattn_setup()
    _L0_xattn_in = {k: v for k, v in _L0_xattn_all.items() if k in ('Wq', 'Wk', 'Wv', 'Wo', 'bo')}
    del _L0_xattn_all

    def _L0_ffn_setup():
        import jax, jax.numpy as jnp
        import numpy as np
        B, S, D, H, F = (4, 512, 128, 16, 512)
        CAP = 0.125
        ROPE_BASE = 10000.0

        def rmsnorm(x, g):
            return x * jax.lax.rsqrt(jnp.mean(x * x, -1, keepdims=True) + 1e-06) * g

        def rope(t, pos):
            hd = t.shape[-1]
            inv = 1.0 / ROPE_BASE ** (jnp.arange(0, hd, 2, dtype=jnp.float32) / hd)
            f = pos[:, None, :, None].astype(jnp.float32) * inv
            emb = jnp.concatenate([f, f], axis=-1)
            cos, sin = (jnp.cos(emb), jnp.sin(emb))
            rot = jnp.concatenate([-t[..., hd // 2:], t[..., :hd // 2]], axis=-1)
            return t * cos + rot * sin
        key = jax.random.key(seed)
        ks = jax.random.split(key, 9)
        scale = 0.02
        x = jax.random.normal(ks[0], (B, S, D), jnp.float32)
        causal = jnp.where(jnp.tril(jnp.ones((S, S), bool)), 0.0, -1000000000.0).astype(jnp.float32)
        attention_mask = jnp.broadcast_to(causal[None, None], (B, 1, S, S))
        position_ids = jnp.broadcast_to(jnp.arange(S, dtype=jnp.int32), (B, S))
        return {'x': x, 'attention_mask': attention_mask, 'position_ids': position_ids, 'router_w': jax.random.normal(ks[1], (D, 1), jnp.float32) * scale, 'router_b': jnp.zeros((1,), jnp.float32), 'wq': jax.random.normal(ks[2], (D, D), jnp.float32) * scale, 'wk': jax.random.normal(ks[3], (D, D), jnp.float32) * scale, 'wv': jax.random.normal(ks[4], (D, D), jnp.float32) * scale, 'wo': jax.random.normal(ks[5], (D, D), jnp.float32) * scale, 'w1': jax.random.normal(ks[6], (D, F), jnp.float32) * scale, 'w2': jax.random.normal(ks[7], (F, D), jnp.float32) * scale, 'ln1': jnp.ones((D,), jnp.float32), 'ln2': jnp.ones((D,), jnp.float32)}
    _L0_ffn_all = _L0_ffn_setup()
    _L0_ffn_in = {k: v for k, v in _L0_ffn_all.items() if k in ('attention_mask', 'position_ids', 'router_w', 'router_b', 'wq', 'wk', 'wv', 'wo', 'w1', 'w2', 'ln1', 'ln2')}
    del _L0_ffn_all
    return {'x': x, 'ctx_768': ctx_768, 'L0_attn_w_q': _L0_attn_in['w_q'], 'L0_attn_b_q': _L0_attn_in['b_q'], 'L0_attn_w_k': _L0_attn_in['w_k'], 'L0_attn_b_k': _L0_attn_in['b_k'], 'L0_attn_w_v': _L0_attn_in['w_v'], 'L0_attn_b_v': _L0_attn_in['b_v'], 'L0_attn_w_out': _L0_attn_in['w_out'], 'L0_attn_b_out': _L0_attn_in['b_out'], 'L0_xattn_Wq': _L0_xattn_in['Wq'], 'L0_xattn_Wk': _L0_xattn_in['Wk'], 'L0_xattn_Wv': _L0_xattn_in['Wv'], 'L0_xattn_Wo': _L0_xattn_in['Wo'], 'L0_xattn_bo': _L0_xattn_in['bo'], 'L0_ffn_attention_mask': _L0_ffn_in['attention_mask'], 'L0_ffn_position_ids': _L0_ffn_in['position_ids'], 'L0_ffn_router_w': _L0_ffn_in['router_w'], 'L0_ffn_router_b': _L0_ffn_in['router_b'], 'L0_ffn_wq': _L0_ffn_in['wq'], 'L0_ffn_wk': _L0_ffn_in['wk'], 'L0_ffn_wv': _L0_ffn_in['wv'], 'L0_ffn_wo': _L0_ffn_in['wo'], 'L0_ffn_w1': _L0_ffn_in['w1'], 'L0_ffn_w2': _L0_ffn_in['w2'], 'L0_ffn_ln1': _L0_ffn_in['ln1'], 'L0_ffn_ln2': _L0_ffn_in['ln2']}

def reference(x, ctx_768, L0_attn_w_q, L0_attn_b_q, L0_attn_w_k, L0_attn_b_k, L0_attn_w_v, L0_attn_b_v, L0_attn_w_out, L0_attn_b_out, L0_xattn_Wq, L0_xattn_Wk, L0_xattn_Wv, L0_xattn_Wo, L0_xattn_bo, L0_ffn_attention_mask, L0_ffn_position_ids, L0_ffn_router_w, L0_ffn_router_b, L0_ffn_wq, L0_ffn_wk, L0_ffn_wv, L0_ffn_wo, L0_ffn_w1, L0_ffn_w2, L0_ffn_ln1, L0_ffn_ln2):
    import jax
    import jax.numpy as jnp

    def _L0_attn_ref(x, w_q, b_q, w_k, b_k, w_v, b_v, w_out, b_out):
        import jax, jax.numpy as jnp
        import numpy as np
        EMBED_DIM = 128
        D = x.shape[-1]
        scaling = 1.0 / jnp.sqrt(jnp.asarray(D, x.dtype))
        q = jnp.einsum('bsd,ed->bse', x, w_q) + b_q
        k = jnp.einsum('bsd,ed->bse', x, w_k) + b_k
        v = jnp.einsum('bsd,ed->bse', x, w_v) + b_v
        scores = jnp.einsum('bqd,bkd->bqk', q, k) * scaling
        attn = jax.nn.softmax(scores, axis=-1)
        out = jnp.einsum('bqk,bkd->bqd', attn, v)
        return jnp.einsum('bsd,ed->bse', out, w_out) + b_out

    def _L0_xattn_ref(x, context, Wq, Wk, Wv, Wo, bo):
        import jax, jax.numpy as jnp
        import numpy as np
        HEADS = 16
        DIM_HEAD = 64
        SCALE = DIM_HEAD ** (-0.5)
        B, Nq, _ = x.shape
        Nc = context.shape[1]
        q = (x @ Wq).reshape(B, Nq, HEADS, DIM_HEAD).transpose(0, 2, 1, 3)
        k = (context @ Wk).reshape(B, Nc, HEADS, DIM_HEAD).transpose(0, 2, 1, 3)
        v = (context @ Wv).reshape(B, Nc, HEADS, DIM_HEAD).transpose(0, 2, 1, 3)
        sim = jnp.einsum('bhid,bhjd->bhij', q, k) * SCALE
        attn = jax.nn.softmax(sim, axis=-1)
        out = jnp.einsum('bhij,bhjd->bhid', attn, v)
        out = out.transpose(0, 2, 1, 3).reshape(B, Nq, HEADS * DIM_HEAD)
        return out @ Wo + bo

    def _L0_ffn_ref(x, attention_mask, position_ids, router_w, router_b, wq, wk, wv, wo, w1, w2, ln1, ln2):
        import jax, jax.numpy as jnp
        import numpy as np
        B, S, D, H, F = (4, 512, 128, 16, 512)
        CAP = 0.125
        ROPE_BASE = 10000.0

        def rmsnorm(x, g):
            return x * jax.lax.rsqrt(jnp.mean(x * x, -1, keepdims=True) + 1e-06) * g

        def rope(t, pos):
            hd = t.shape[-1]
            inv = 1.0 / ROPE_BASE ** (jnp.arange(0, hd, 2, dtype=jnp.float32) / hd)
            f = pos[:, None, :, None].astype(jnp.float32) * inv
            emb = jnp.concatenate([f, f], axis=-1)
            cos, sin = (jnp.cos(emb), jnp.sin(emb))
            rot = jnp.concatenate([-t[..., hd // 2:], t[..., :hd // 2]], axis=-1)
            return t * cos + rot * sin
        b, s, d = x.shape
        hd = d // H
        weights = (x @ router_w)[..., 0] + router_b[0]
        k = int(CAP * s)
        topv, topi = jax.lax.top_k(weights, k)
        thr = topv[:, -1]
        sel_mask = (weights > thr[:, None]).astype(x.dtype)
        kc = k - 1
        sel_idx = jnp.sort(topi[:, :kc], axis=1)
        bidx = jnp.arange(b)[:, None]
        x_sel = x[bidx, sel_idx]
        pos_sel = position_ids[bidx, sel_idx]
        w_sel = weights[bidx, sel_idx]
        m = attention_mask[:, 0]
        m_sel = m[bidx[:, :, None], sel_idx[:, :, None], sel_idx[:, None, :]]
        hn = rmsnorm(x_sel, ln1)

        def heads(t):
            return t.reshape(b, kc, H, hd).transpose(0, 2, 1, 3)
        q = rope(heads(hn @ wq), pos_sel)
        kk = rope(heads(hn @ wk), pos_sel)
        v = heads(hn @ wv)
        sc = jnp.einsum('bhqd,bhkd->bhqk', q, kk) / np.sqrt(hd).astype(np.float32)
        sc = sc + m_sel[:, None]
        a = jax.nn.softmax(sc, axis=-1)
        o = jnp.einsum('bhqk,bhkd->bhqd', a, v).transpose(0, 2, 1, 3).reshape(b, kc, d) @ wo
        x1 = x_sel + o
        x2 = x1 + jax.nn.gelu(rmsnorm(x1, ln2) @ w1) @ w2
        proc = x2 * w_sel[..., None]
        out = jnp.zeros_like(x).at[bidx, sel_idx].set(proc)
        return out + x * (1.0 - sel_mask)[..., None]
    x = x + _L0_attn_ref(_layernorm(x, axis=-1), L0_attn_w_q, L0_attn_b_q, L0_attn_w_k, L0_attn_b_k, L0_attn_w_v, L0_attn_b_v, L0_attn_w_out, L0_attn_b_out)
    x = x + _L0_xattn_ref(_layernorm(x, axis=-1), ctx_768, L0_xattn_Wq, L0_xattn_Wk, L0_xattn_Wv, L0_xattn_Wo, L0_xattn_bo)
    x = x + _L0_ffn_ref(_layernorm(x, axis=-1), L0_ffn_attention_mask, L0_ffn_position_ids, L0_ffn_router_w, L0_ffn_router_b, L0_ffn_wq, L0_ffn_wk, L0_ffn_wv, L0_ffn_wo, L0_ffn_w1, L0_ffn_w2, L0_ffn_ln1, L0_ffn_ln2)
    return x

_drawn_inputs = setup_inputs


def setup_inputs(seed=0):
    import zlib

    import numpy as np

    out = dict(_drawn_inputs(seed))
    spreads = {'L0_xattn_bo': (0.0, 0.1), 'L0_ffn_ln1': (1.0, 0.6), 'L0_ffn_ln2': (1.0, 0.6)}
    factors = {'L0_attn_w_q': 2.787,
     'L0_attn_b_q': 8.0,
     'L0_attn_w_k': 2.882,
     'L0_attn_b_k': 8.0,
     'L0_ffn_wq': 8.0,
     'L0_ffn_wk': 8.0,
     'L0_ffn_wv': 8.0,
     'L0_ffn_wo': 8.0,
     'L0_ffn_w1': 8.0,
     'L0_ffn_w2': 8.0}
    for name, (base, spread) in spreads.items():
        noise = np.random.default_rng([zlib.crc32(name.encode()), seed]).standard_normal(out[name].shape)
        drawn = base * np.exp(spread * noise) if base else spread * noise
        out[name] = jnp.asarray(drawn.astype(out[name].dtype))
    for name, factor in factors.items():
        out[name] = (out[name] * factor).astype(out[name].dtype)
    return out
```

```python
from contextlib import ExitStack

import numpy as np

import concourse.bass as bass
from concourse import mybir

F32 = mybir.dt.float32
BF16 = mybir.dt.bfloat16
I32 = mybir.dt.int32
ALU = mybir.AluOpType
ACT = mybir.ActivationFunctionType
AX_X = mybir.AxisListType.X

P = 128
B, S, D = 16, 256, 128
T = S // P
NC, DC = 1601, 96
H, DH = 16, 64
KT = 13
KP = -(-NC // KT)
KFULL = NC - (KP - 1) * KT
HP = H // 2
W2 = 2 * S
TILES = HP * KT
F = 512
FH, FD = 16, 8
CAP = S // 8
NSEL = CAP - 1
MB, MS = 4, 512
NG = B // 4
LN_EPS, RMS_EPS = 1e-5, 1e-6
ROPE_BASE = 10000.0
PRING = 8
AV_LAG = 4


class Mark:

    def __init__(self, sem, value):
        self.sem, self.value = sem, value


class Engine:

    def __init__(self, eng, sem):
        self.eng, self.sem, self.n, self.seen = eng, sem, 0, {}

    def did(self, ins):
        self.n += 1
        ins.then_inc(self.sem, 1)
        return Mark(self.sem, self.n)

    def wait(self, *marks):
        for m in marks:
            if m is not None and self.seen.get(id(m.sem), 0) < m.value:
                self.eng.wait_ge(m.sem, m.value)
                self.seen[id(m.sem)] = m.value


class Arrival:

    def __init__(self, sem):
        self.sem, self.n = sem, 0

    def of(self, dma):
        self.n += 16
        dma.then_inc(self.sem, 16)
        return Mark(self.sem, self.n)


def build(nc, a, out):
    with ExitStack() as ctx:

        regions = [ctx.enter_context(ExitStack())]

        def sb(name, shape, dt=F32):
            return regions[-1].enter_context(nc.sbuf_tensor(name, shape, dt))

        def sem(name):
            return ctx.enter_context(nc.semaphore(name))

        PE = Engine(nc.tensor, sem("pe_steps"))
        AC = Engine(nc.scalar, sem("act_steps"))
        VE = Engine(nc.vector, sem("dve_steps"))
        PO = Engine(nc.gpsimd, sem("pool_steps"))
        SP = Engine(nc.sync, sem("sp_steps"))
        pe, act, dve, pool, sp = PE.eng, AC.eng, VE.eng, PO.eng, SP.eng
        arrival = {}

        def load(key, dst, src, eng=sp):
            if key not in arrival:
                arrival[key] = Arrival(sem("in_" + key))
            return arrival[key].of(eng.dma_start(dst, src))

        PS = ctx.enter_context(nc.psum_tensor("PS", [P, 8, 512], F32))

        ident = sb("ident", [P, P])
        identb = sb("identb", [P, P], BF16)
        minus_half = sb("minus_half", [P, 8])
        lower = sb("lower", [P, T, T, P])
        slots = sb("slots", [P, CAP])
        sloti = sb("sloti", [P, CAP], I32)
        headmask = sb("headmask", [P, FH])
        blockmask = sb("blockmask", [P, 32])
        inv_freq = sb("inv_freq", [P, FD // 2])

        wqT = sb("wqT", [P, P])
        wkT = sb("wkT", [P, P])
        wv = sb("wv", [P, P])
        woutT = sb("woutT", [P, P])
        wvo = sb("wvo", [P, P])
        cols = sb("cols", [P, 3])
        brow = sb("brow", [P, P])
        xbo = sb("xbo", [P, P])
        crow = sb("crow", [P, P])
        big = {n: (n, [P, HP, D if n in ("xWqT", "xWo") else DC]) for n in ("xWqT", "xWkT", "xWvT", "xWo")}
        fwq = sb("fwq", [P, 2, P])
        fwv = sb("fwv", [P, P])
        fwo = sb("fwo", [P, P])
        fw1 = sb("fw1", [P, F])
        fw2 = sb("fw2", [P, F // P, P])
        ln1r = sb("ln1r", [P, P])
        ln2r = sb("ln2r", [P, P])
        rwr = sb("rwr", [P, P])
        rbc = sb("rbc", [P, 1])
        posi = sb("posi", [P, MB, T], I32)
        msk = sb("msk", [P, MB, T, S])

        X = sb("X", [P, B * T, D])
        X3 = sb("X3", [P, B * T, D + 2])
        GT = sb("GT", [P, B * T, CAP])

        x_dram = a["x"].rearrange("b (p t) d -> p b t d", t=T)
        X4 = X[:, :, :].rearrange("p (b t) d -> p b t d", t=T)
        NPAIR = B // 2
        x_in = []
        for pr in range(NPAIR):
            x_in.append(load(f"x{pr}", X4[:, 2 * pr:2 * pr + 2, :, :], x_dram[:, 2 * pr:2 * pr + 2, :, :]))
            if pr == 0:
                for n, t in (("w_qT", wqT), ("w_kT", wkT), ("w_v", wv), ("w_outT", woutT)):
                    w_in = load("w", t[:, :], a[n], act)
                for i, n in enumerate(("b_q", "b_k", "b_v")):
                    w_in = load("w", cols[:, i:i + 1], a[n].rearrange("(p o) -> p o", o=1), act)
                for n, t in (("b_out", brow), ("xbo", xbo), ("ln1", ln1r), ("ln2", ln2r)):
                    w_in = load("w", t[:, :], a[n].rearrange("(o n) -> o n", o=1).to_broadcast([P, P]), act)
                w_in = load("w", rwr[:, :], a["router_w"].rearrange("n o -> o n").to_broadcast([P, P]), act)
                w_in = load("w", rbc[:, :], a["router_b"].rearrange("(o n) -> o n", o=1).to_broadcast([P, 1]), act)
        stats = sb("stats", [P, 4, 6])
        mv = sb("mv", [P, 2, 4, 2])
        rstd = sb("rstd", [P, 2, 4])
        junk = sb("junk", [P, 8, S], BF16)
        cnt = sb("cnt", [P, 2, 3, T])
        wraw = sb("wraw", [P, 2, T])
        keep = sb("keep", [P, 2, T])
        rank = sb("rank", [P, 2, T])

        regions.append(ctx.enter_context(ExitStack()))
        X2T = sb("X2T", [P, B, S])
        G = sb("G", [P, H, DC])
        M = sb("M", [DC + 1, H, D + 1])
        rxa = sb("rxa", [P, 2, T])
        Cf = sb("Cf", [KP, KT, DC])
        Ch = [sb(f"Ch{i}", [KP, KT, DC + 1], BF16) for i in range(2)]
        Cl = [sb(f"Cl{i}", [KP, KT, DC], BF16) for i in range(2)]
        ChT = [sb(f"ChT{i}", [DC + 2, KT, KP], BF16) for i in range(2)]
        ClT = [sb(f"ClT{i}", [DC, KT, KP], BF16) for i in range(2)]
        AH = [sb(f"AH{i}", [DC + 2, H * S], BF16) for i in range(2)]
        AL = [sb(f"AL{i}", [DC, H * S], BF16) for i in range(2)]
        U = [sb(f"U{i}", [DC + 1, W2]) for i in range(2)]
        pmax = sb("pmax", [P, 2, H * T, 2])
        nmax = sb("nmax", [P, 2, H * T])
        mh = sb("mh", [H * T, P], BF16)
        ml = sb("ml", [H * T, P], BF16)

        regions.append(ctx.enter_context(ExitStack()))
        big = {n: sb(*v) for n, v in big.items()}
        for n in big:
            big_in = load("xw", big[n][:, :, :], a[n].rearrange("(j p) n -> p j n", p=P), act)
        xn = sb("xn", [P, 2, 4, D])
        xT = sb("xT", [P, 2, W2])
        qT = sb("qT", [P, 2, W2])
        kT = sb("kT", [P, 2, W2])
        vp = sb("vp", [P, 2, 4, D])
        nm = sb("nm", [P, 2, 4])
        den = sb("den", [P, 2, 4])
        rden = sb("rden", [P, 2, 4])
        ex = sb("ex", [P, 2, T, S])
        exT = sb("exT", [P, 2, T, T, P])
        xn2 = sb("xn2", [P, 2, 4, D])

        def load_context(b):
            c = a["ctx_768"]
            last = (KP - 1) * KT
            sp_wait = (c_split.get(b - 1),)
            SP.wait(*sp_wait)
            load("ctx", Cf[0:KP - 1, :, :], c[b, 0:last, :].rearrange("(p t) d -> p t d", t=KT))
            load("ctx", Cf[KP - 1:KP, 0:KFULL, :],
                 c[b, last:NC, :].rearrange("(o t) d -> o t d", o=1))
            return load("ctx", Cf[KP - 1:KP, KFULL:KT, :],
                        c[b, NC - (KT - KFULL):NC, :].rearrange("(o t) d -> o t d", o=1))

        c_split = {}
        ctx_in = {0: load_context(0)}
        for n, t in (("wq", fwq[:, 0, :]), ("wk", fwq[:, 1, :]), ("wv", fwv[:, :]), ("wo", fwo[:, :]),
                     ("w1", fw1[:, :]), ("w2", fw2[:, :, :])):
            src = a["f" + n]
            fw_in = load("fw", t, src.rearrange("(j p) n -> p j n", p=P) if n == "w2" else src)
        fw_in = load("fw", posi[:, :, :], a["position_ids"][:, 0:S].rearrange("b (p t) -> p b t", t=T))
        for mb in range(MB):
            fw_in = load("fw", msk[:, mb, :, :],
                         a["attention_mask"][mb, 0, 0:S, 0:S].rearrange("(p t) n -> p t n", t=T))

        def const(ins):
            m = PO.did(ins)
            PO.wait(m)
            return m

        const(pool.memset(ident[:, :], 0.0))
        const(pool.memset(identb[:, :], 0.0))
        const(pool.memset(lower[:, :, :, :], 1.0))
        m0 = const(pool.memset(headmask[:, :], 1.0))
        m0 = const(pool.memset(blockmask[:, :], 1.0))
        PO.wait(m0)
        for t in (ident, identb):
            ident_ready = const(pool.affine_select(out=t[:, :], in_=t[:, :], compare_op=ALU.not_equal, fill=1.0,
                                                    base=0, pattern=[[-1, P]], channel_multiplier=1))
        consts = const(pool.memset(minus_half[:, :], -0.5))
        for i in range(FD // 2):
            inv = float(np.float32(1.0) / np.power(np.float32(ROPE_BASE), np.float32(2 * i / FD)))
            const(pool.memset(inv_freq[:, i:i + 1], inv))
        for t in range(T):
            const(pool.affine_select(out=lower[:, t, :, :], in_=lower[:, t, :, :], compare_op=ALU.is_gt, fill=0.0,
                                      base=t, pattern=[[-1, T], [-T, P]], channel_multiplier=T))
        m1 = const(pool.affine_select(out=headmask[:, :], in_=headmask[:, :], compare_op=ALU.is_ge, fill=0.0,
                                       base=0, pattern=[[-FD, FH]], channel_multiplier=1))
        m2 = const(pool.affine_select(out=blockmask[:, :].rearrange("p (h d) -> p h d", d=FD),
                                       in_=blockmask[:, :].rearrange("p (h d) -> p h d", d=FD),
                                       compare_op=ALU.is_ge, fill=0.0,
                                       base=0, pattern=[[-32, 4], [0, FD]], channel_multiplier=1))
        PO.wait(m1, m2)
        const(pool.affine_select(out=headmask[:, :], in_=headmask[:, :], compare_op=ALU.is_ge, fill=0.0,
                                  base=FD - 1, pattern=[[FD, FH]], channel_multiplier=-1))
        const(pool.affine_select(out=blockmask[:, :].rearrange("p (h d) -> p h d", d=FD),
                                  in_=blockmask[:, :].rearrange("p (h d) -> p h d", d=FD),
                                  compare_op=ALU.is_ge, fill=0.0,
                                  base=31, pattern=[[32, 4], [0, FD]], channel_multiplier=-1))
        m3 = const(pool.iota(sloti[:, :], pattern=[[1, CAP]], base=0, channel_multiplier=0))
        PO.wait(m3)
        m4 = const(pool.tensor_copy(slots[:, :], sloti[:, :]))
        PO.wait(m4)
        const(pool.memset(slots[:, NSEL:CAP], -1.0))
        for i in range(2):
            const(pool.memset(ChT[i][DC:DC + 2, :, :], 1.0))
            const(pool.memset(Ch[i][:, :, DC:DC + 1], 1.0))
        m5 = const(pool.memset(M[:, :, :], 0.0))
        PO.wait(m5)
        consts = const(pool.memset(M[DC:DC + 1, :, D:D + 1], 1.0))

        def rsqrt(dst, var, n, scale, eps, after):
            PO.wait(after)
            m = PO.did(pool.tensor_scalar(dst, var, scale, eps, ALU.mult, ALU.add))
            PO.wait(m)
            return PO.did(pool.tensor_tensor(dst, dst, minus_half[:, 0:n], ALU.pow))

        PE.wait(w_in, ident_ready)
        pe.matmul(PS[:, 0, 0:P], wv[:, :], woutT[:, :], start=True, stop=True)
        made = PE.did(pe.matmul(PS[:, 1, 0:P], cols[:, 2:3].to_broadcast([P, P]), woutT[:, :], start=True, stop=True))
        VE.wait(made, w_in)
        VE.did(dve.tensor_copy(wvo[:, :], PS[:, 0, 0:P]))
        wvo_ready = VE.did(dve.tensor_tensor(crow[:, :], PS[:, 1, 0:P], brow[:, :], ALU.add))
        PE.wait(big_in, wvo_ready)
        G2 = G[:, :, :].rearrange("p (j e) c -> p e j c", e=2)
        M2 = M[:, :, :].rearrange("p (j e) c -> p e j c", e=2)
        for q in range(2):
            banks = ((2, 3, 4, 5), (6, 7, 0, 1))[q]
            for even in range(2):
                r = slice(DH * even, DH * even + DH)
                for j in range(4):
                    c = j * P
                    pe.matmul(PS[:, banks[even], c:c + DC], big["xWqT"][r, 4 * q + j, :], big["xWkT"][r, 4 * q + j, :],
                              start=True, stop=True)
                    mm = pe.matmul(PS[0:DC, banks[2 + even], c:c + D], big["xWvT"][r, 4 * q + j, :],
                                   big["xWo"][r, 4 * q + j, :], start=True, stop=True)
            made = PE.did(mm)
            AC.wait(made)
            VE.wait(made, consts)
            for even in range(2):
                g4 = PS[:, banks[even], :].rearrange("p (h c) -> p h c", c=P)[:, :, 0:DC]
                m4_ = PS[0:DC, banks[2 + even], :].rearrange("p (h c) -> p h c", c=P)
                g_done = AC.did(act.activation(G2[:, even, 4 * q:4 * q + 4, :], g4, ACT.Copy, scale=DH ** -0.5))
                m_done = VE.did(dve.tensor_copy(M2[0:DC, even, 4 * q:4 * q + 4, 0:D], m4_))
        weights_done = (g_done, m_done)

        ln_turn = [0]
        ln_last = {}

        def layernorm(x_of, dst_of, n, after):
            i = ln_turn[0] % 2
            ln_turn[0] += 1
            VE.wait(*after)
            VE.wait(ln_last.get("stats"), ln_last.get(i))
            for k in range(n):
                m = VE.did(dve.bn_stats(stats[:, k, :], x_of(k)))
            VE.wait(m)
            for k in range(n):
                m = VE.did(dve.bn_aggr(mv[:, i, k, :], stats[:, k, :]))
            ln_last["stats"] = m
            r = rsqrt(rstd[:, i, 0:n], mv[:, i, 0:n, 1], n, 1.0, LN_EPS, m)
            VE.wait(r)
            for k in range(n):
                m = VE.did(dve.tensor_scalar(dst_of(k), x_of(k), mv[:, i, k, 0:1], rstd[:, i, k:k + 1],
                                             ALU.subtract, ALU.mult))
            ln_last[i] = m
            return m

        st = [dict() for _ in range(NPAIR + 6)]
        SA_SCALE = float(D) ** -0.5

        def g(p, k):
            return st[p].get(k) if p >= 0 else None

        def sa_norm(p):
            i = p % 2
            st[p]["xn"] = layernorm(lambda k: X[:, 4 * p + k, :], lambda k: xn[:, i, k, :], 4,
                                    (x_in[p], g(p - 2, "xT_made")))

        def sa_project(p):
            i = p % 2
            PE.wait(st[p]["xn"], ident_ready, *weights_done, g(p - 1, "xT"), g(p - 1, "x2T_ev"))
            for k in range(4):
                m = pe.transpose(PS[:, 0, k * P:(k + 1) * P], xn[:, i, k, :], ident[:, :])
            st[p]["xT_made"] = PE.did(m)
            AC.wait(st[p]["xT_made"], g(p - 2, "v_made"))
            st[p]["xT"] = AC.did(act.activation(xT[:, i, :], PS[:, 0, :], ACT.Copy))
            PE.wait(st[p]["xT"], w_in, wvo_ready,
                    g(p - 1, "q"), g(p - 1, "k"), g(p - 1, "v"))
            q_made = PE.did(pe.matmul(PS[:, 1, :], wqT[:, :], xT[:, i, :], start=True, stop=True))
            k_made = PE.did(pe.matmul(PS[:, 2, :], wkT[:, :], xT[:, i, :], start=True, stop=True))
            for k in range(4):
                m = pe.matmul(PS[:, 3, k * P:(k + 1) * P], xT[:, i, k * P:(k + 1) * P], wvo[:, :], start=True, stop=True)
            st[p]["v_made"] = PE.did(m)
            AC.wait(q_made, g(p - 2, "s_made"))
            st[p]["q"] = AC.did(act.activation(qT[:, i, :], PS[:, 1, :], ACT.Identity, bias=cols[:, 0:1]))
            VE.wait(k_made, g(p - 2, "s_made"))
            st[p]["k"] = VE.did(dve.tensor_scalar(kT[:, i, :], PS[:, 2, :], cols[:, 1:2], None, ALU.add))
            VE.wait(st[p]["v_made"], g(p - 2, "o_made"))
            st[p]["v"] = VE.did(dve.tensor_copy(vp[:, i, :, :], PS[:, 3, :].rearrange("p (k d) -> p k d", d=D)))

        def sa_scores(p):
            i = p % 2
            PE.wait(st[p]["q"], st[p]["k"])
            for j in range(2):
                PE.wait(g(p - 1, f"ex{j}"))
                for t in range(T):
                    c = j * S + t * P
                    m = pe.matmul(PS[:, 4 + j, t * S:(t + 1) * S], qT[:, i, c:c + P], kT[:, i, j * S:(j + 1) * S],
                                  start=True, stop=True)
                st[p]["s_made"] = PE.did(m)
                VE.wait(st[p]["s_made"], g(p - 2, f"ex{j}"))
                m = VE.did(dve.tensor_reduce(nm[:, i, 2 * j:2 * j + 2],
                                             PS[:, 4 + j, :].rearrange("p (t n) -> p t n", n=S), AX_X, ALU.max,
                                             negate=True))
                PO.wait(m)
                m = PO.did(pool.tensor_scalar(nm[:, i, 2 * j:2 * j + 2], nm[:, i, 2 * j:2 * j + 2], SA_SCALE, 0.0,
                                              ALU.mult, ALU.add))
                AC.wait(m, g(p - 1, f"exT_made{j}"), g(p - 2, "x1"))
                for t in range(T):
                    k = 2 * j + t
                    m = AC.did(act.activation(ex[:, j, t, :], PS[:, 4 + j, t * S:(t + 1) * S], ACT.Exp,
                                              bias=nm[:, i, k:k + 1], scale=SA_SCALE, accum_out=den[:, i, k:k + 1]))
                st[p][f"ex{j}"] = m

        def sa_output(p):
            i = p % 2
            for j in range(2):
                PE.wait(st[p][f"ex{j}"], g(p - 1 if j == 0 else p, "exT"))
                for kt in range(T):
                    for t in range(T):
                        c = (kt * T + t) * P
                        m = pe.transpose(PS[:, 6, c:c + P], ex[:, j, t, kt * P:(kt + 1) * P], ident[:, :])
                st[p][f"exT_made{j}"] = PE.did(m)
                AC.wait(st[p][f"exT_made{j}"], g(p - 1, "o_made"))
                st[p]["exT"] = AC.did(act.activation(exT[:, j, :, :, :],
                                                     PS[:, 6, :].rearrange("p (k t q) -> p k t q", k=T, t=T), ACT.Copy))
                PE.wait(st[p]["exT"], st[p]["v"], g(p - 1, "x1"))
                for t in range(T):
                    for kt in range(T):
                        m = pe.matmul(PS[:, 7, (2 * j + t) * P:(2 * j + t + 1) * P], exT[:, j, kt, t, :],
                                      vp[:, i, 2 * j + kt, :], start=(kt == 0), stop=(kt == T - 1))
                st[p]["o_made"] = PE.did(m)
            PO.wait(st[p]["xn"], wvo_ready)
            for k in range(4):
                m = PO.did(pool.tensor_tensor(X[:, 4 * p + k, :], X[:, 4 * p + k, :], crow[:, :], ALU.add))
            VE.wait(st[p]["ex1"], g(p - 2, "x1"))
            r = VE.did(dve.reciprocal(rden[:, i, :], den[:, i, :]))
            VE.wait(st[p]["o_made"], m, r)
            for k in range(4):
                m = VE.did(dve.scalar_tensor_tensor(out=X[:, 4 * p + k, :], in0=PS[:, 7, k * P:(k + 1) * P],
                                                    scalar=rden[:, i, k:k + 1], in1=X[:, 4 * p + k, :],
                                                    op0=ALU.mult, op1=ALU.add))
            st[p]["x1"] = m

        def sa_norm2(p):
            i = p % 2
            m = layernorm(lambda k: X[:, 4 * p + k, :], lambda k: xn2[:, i, k, :], 4,
                          (st[p]["x1"], g(p - 2, "x2T_made")))
            PO.wait(m)
            for k in range(4):
                st[p]["bo"] = PO.did(pool.tensor_tensor(X[:, 4 * p + k, :], X[:, 4 * p + k, :], xbo[:, :], ALU.add))
            PE.wait(m, g(min(p + 3, NPAIR - 1), "xT"), g(p - 1, "x2T_ev"))
            for k in range(4):
                m = pe.transpose(PS[:, 0, k * P:(k + 1) * P], xn2[:, i, k, :], ident[:, :])
            st[p]["x2T_made"] = PE.did(m)
            AC.wait(st[p]["x2T_made"])
            m = AC.did(act.activation(X2T[:, 2 * p:2 * p + 2, :],
                                      PS[:, 0, :].rearrange("p (b s) -> p b s", s=S), ACT.Copy))
            st[p]["x2T_ev"] = m
            return m

        x2T_ready = {}
        for s in range(NPAIR + 3):
            if s >= 3:
                x2T_ready[s - 3] = sa_norm2(s - 3)
            if s < NPAIR:
                sa_norm(s)
            if 0 <= s - 2 < NPAIR:
                sa_output(s - 2)
            if 0 <= s - 1 < NPAIR:
                sa_scores(s - 1)
            if s < NPAIR:
                sa_project(s)

        regions.pop().close()
        PF = sb("PF", [KP, PRING, W2])
        PL = sb("PL", [KP, PRING, W2], BF16)
        PH = PF[:, :, :].bitcast(BF16).rearrange("p r (n w) -> p r n w", w=2)[:, :, :, 1]
        MAXB = {0: 0, 1: 2}
        NQ = 4
        NKEY = KT * KP // NQ
        small_free = [st[NPAIR - 1]["x1"]]
        max_free = {0: st[NPAIR - 1]["x2T_ev"], 1: st[NPAIR - 1]["v"]}
        max_free[0] = [st[NPAIR - 1]["x2T_ev"], st[NPAIR - 1]["q"], st[NPAIR - 1]["k"]]
        max_free[1] = [st[NPAIR - 1]["v"], st[NPAIR - 1]["k"]]
        st_free = {0: st[NPAIR - 1]["ex0"], 1: st[NPAIR - 1]["ex1"]}
        acc_free = [st[NPAIR - 1]["exT"]]
        av_done, exp_done, lo_done = {}, {}, {}
        u_free = {0: None, 1: None}
        max_used, st_used, av_used = {}, {}, {}
        x_marks = {}

        def split_context(b):
            i = b % 2
            PO.wait(ctx_in[b], av_used.get(b - 2), c_tr.get(b - 2))
            m = PO.did(pool.tensor_copy(Ch[i][:, :, 0:DC], Cf[:, :, :]))
            PO.wait(m)
            c_split[b] = PO.did(pool.tensor_tensor(Cl[i][:, :, :], Cf[:, :, :], Ch[i][:, :, 0:DC], ALU.subtract))

        c_tr, c_ready = {}, {}

        def transpose_context(b, part, t0, t1):
            i = b % 2
            src, dst = (Ch, ChT) if part == 0 else (Cl, ClT)
            bank = PS[0:DC, 7, :].bitcast(BF16)
            PE.wait(c_split[b], small_free[0], ident_ready)
            for t in range(t0, t1):
                m = pe.transpose(bank[:, (t - t0) * KP:(t - t0 + 1) * KP], src[i][:, t, 0:DC], identb[0:KP, 0:KP])
            c_tr[b] = PE.did(m)
            AC.wait(c_tr[b], st_used.get(b - 2), consts)
            m = AC.did(act.activation(dst[i][0:DC, t0:t1, :],
                                      bank[:, 0:(t1 - t0) * KP].rearrange("p (t k) -> p t k", k=KP), ACT.Copy))
            small_free[0] = c_ready[b] = m

        a_ready = {}

        def make_queries(b, hp):
            i = b % 2
            PE.wait(x2T_ready[b // 2], small_free[0], g_done)
            for j in range(2):
                m = pe.matmul(PS[0:DC, 7, j * S:(j + 1) * S], G[:, 2 * hp + j, :], X2T[:, b, :], start=True, stop=True)
            m = PE.did(m)
            cols_ = slice(hp * W2, (hp + 1) * W2)
            AC.wait(m, st_used.get(b - 2))
            hi = AC.did(act.activation(AH[i][0:DC, cols_], PS[0:DC, 7, :], ACT.Copy))
            VE.wait(hi)
            m = VE.did(dve.tensor_tensor(AL[i][:, cols_], PS[0:DC, 7, :], AH[i][0:DC, cols_], ALU.subtract))
            small_free[0] = a_ready[(b, hp)] = m

        def max_chunk(b, ht, half):
            i, k = b % 2, (2 * ht + half) % 2
            PE.wait(c_ready[b], a_ready[(b, ht // 4)], *max_free[k])
            keys = ChT[i][0:DC, :, :].rearrange("p t k -> p (t k)")
            for n in range(2):
                c = (2 * half + n) * NKEY
                m = pe.matmul(PS[:, MAXB[k] + n, 0:NKEY], AH[i][0:DC, ht * P:(ht + 1) * P], keys[:, c:c + NKEY],
                              start=True, stop=True)
            m = PE.did(m)
            max_used[b] = m
            VE.wait(m)
            m = VE.did(dve.tensor_reduce(pmax[:, i, ht, half:half + 1], PS[:, MAXB[k]:MAXB[k] + 2, 0:NKEY],
                                         mybir.AxisListType.XY, ALU.max))
            max_free[k] = [m]
            x_marks["pmax"] = m

        m_in = {}

        def finish_max(b):
            i = b % 2
            VE.wait(x_marks["pmax"])
            m = VE.did(dve.tensor_reduce(nmax[:, i, :], pmax[:, i, :, :], AX_X, ALU.max, negate=True))
            PE.wait(m, small_free[0])
            m = PE.did(pe.transpose(PS[0:H * T, 7, 0:P], nmax[:, i, :], ident[:, :]))
            AC.wait(m, m_in.get(b - 1))
            hi = AC.did(act.activation(mh[:, :], PS[0:H * T, 7, 0:P], ACT.Copy))
            VE.wait(hi, m_in.get(b - 1))
            lo = VE.did(dve.tensor_tensor(ml[:, :], PS[0:H * T, 7, 0:P], mh[:, :], ALU.subtract))
            small_free[0] = lo
            SP.wait(hi, lo, st_used.get(b - 2))
            load("negmax", AH[i][DC:DC + 1, :], mh[:, :])
            m_in[b] = load("negmax", AH[i][DC + 1:DC + 2, :], ml[:, :])

        def scores_tile(n):
            b, hp, t = n // TILES, n % TILES // KT, n % KT
            i, k, r = b % 2, n % 2, n % PRING
            cols_ = slice(hp * W2, (hp + 1) * W2)
            PE.wait(m_in[b], a_ready[(b, hp)], c_ready[b], st_free[k])
            o = PS[0:KP, 4 + k, :]
            pe.matmul(o, ChT[i][:, t, :], AH[i][:, cols_], start=True, stop=False)
            pe.matmul(o, ChT[i][0:DC, t, :], AL[i][:, cols_], start=False, stop=False)
            m = PE.did(pe.matmul(o, ClT[i][:, t, :], AH[i][0:DC, cols_], start=False, stop=True))
            st_used[b] = m
            AC.wait(m, av_done.get(n - PRING))
            exp_done[n] = st_free[k] = AC.did(act.activation(PF[:, r, :], o, ACT.Exp))
            if n % 2:
                VE.wait(exp_done[n], av_done.get(n - PRING))
                lo_done[n] = lo_done[n - 1] = VE.did(dve.tensor_tensor(
                    PL[:, r - 1:r + 1, :], PF[:, r - 1:r + 1, :], PH[:, r - 1:r + 1, :], ALU.subtract))

        def values_tile(n):
            b, hp, t = n // TILES, n % TILES // KT, n % KT
            i, r = b % 2, n % PRING
            rows = KP if t < KFULL else KP - 1
            PE.wait(exp_done[n], c_split[b])
            if t == 0:
                PE.wait(acc_free[0])
            c_hi, c_lo = Ch[i][0:rows, t, :], Cl[i][0:rows, t, :]
            pe.matmul(PS[0:DC + 1, 6, :], c_hi, PH[0:rows, r, :], start=(t == 0), stop=False)
            pe.matmul(PS[0:DC, 6, :], c_lo, PH[0:rows, r, :], start=False, stop=False)
            PE.wait(lo_done[n])
            m = PE.did(pe.matmul(PS[0:DC + 1, 6, :], c_hi, PL[0:rows, r, :], start=False, stop=(t == KT - 1)))
            av_done[n] = av_used[b] = m
            if t == KT - 1:
                k = (b * HP + hp) % 2
                AC.wait(m, u_free[k])
                acc_free[0] = u_ready[(b, hp)] = AC.did(act.activation(U[k][:, :], PS[0:DC + 1, 6, :], ACT.Copy))

        u_ready, x2_ready = {}, {}

        def project_head(b, h):
            k = (b * HP + h // 2) % 2
            PE.wait(u_ready[(b, h // 2)], small_free[0], m_done)
            for t in range(T):
                c = (h % 2) * S + t * P
                m = pe.matmul(PS[:, 7, t * (D + 1):(t + 1) * (D + 1)], U[k][:, c:c + P], M[:, h, :],
                              start=True, stop=True)
            m = PE.did(m)
            u_free[k] = m
            o = PS[:, 7, 0:T * (D + 1)].rearrange("p (t n) -> p t n", n=D + 1)
            VE.wait(m, x_marks.get(("acc", h % 2)))
            m = VE.did(dve.reciprocal(rxa[:, h % 2, :], o[:, :, D]))
            VE.wait(m, x_marks.get("acc"), st[b // 2]["bo"])
            for t in range(T):
                m = VE.did(dve.scalar_tensor_tensor(out=X[:, T * b + t, :], in0=o[:, t, 0:D],
                                                    scalar=rxa[:, h % 2, t:t + 1], in1=X[:, T * b + t, :],
                                                    op0=ALU.mult, op1=ALU.add))
            small_free[0] = x_marks["acc"] = x_marks[("acc", h % 2)] = x2_ready[b] = m

        sel_steps = {}

        def select_norm(b):
            m = layernorm(lambda k: X[:, T * b + k, :], lambda k: X3[:, T * b + k, 0:D], T, (x2_ready[b],))
            VE.wait(m, w_in, fw_in)
            for t in range(T):
                m = VE.did(dve.tensor_tensor_reduce(out=junk[:, 6 + t, 0:D], in0=X3[:, T * b + t, 0:D], in1=rwr[:, :],
                                                    scale=1.0, scalar=0.0, op0=ALU.mult, op1=ALU.add,
                                                    accum_out=wraw[:, b % 2, t:t + 1]))
            VE.wait(m)
            VE.did(dve.tensor_copy(X3[:, T * b:T * b + T, D + 1], posi[:, min(b, MB - 1), :]))
            m = VE.did(dve.tensor_scalar(X3[:, T * b:T * b + T, D], wraw[:, b % 2, :], rbc[:, 0:1], None, ALU.add))
            PE.wait(m, small_free[0])
            for t in range(T):
                m = pe.transpose(PS[:, 7, t * P:(t + 1) * P], X3[:, T * b + t, D:D + 1].to_broadcast([P, P]),
                                 ident[:, :])
            sel_steps["row"] = PE.did(m)

        def select_rank(b):
            i = b % 2
            row = PS[:, 7, 0:S]
            VE.wait(sel_steps["row"], consts)
            for t in range(T):
                w = X3[:, T * b + t, D:D + 1]
                for j, op in enumerate((ALU.is_gt, ALU.is_ge)):
                    VE.did(dve.tensor_scalar(junk[:, 2 * t + j, :], row, w, None, op, ALU.add,
                                             accum_out=cnt[:, i, j, t:t + 1]))
                m = VE.did(dve.scalar_tensor_tensor(out=junk[:, 4 + t, :], in0=row, scalar=w,
                                                    in1=lower[:, t, :, :].rearrange("p u q -> p (u q)"),
                                                    op0=ALU.is_equal, op1=ALU.mult, accum_out=cnt[:, i, 2, t:t + 1]))
            small_free[0] = m
            VE.wait(m)
            VE.did(dve.tensor_tensor(rank[:, i, :], cnt[:, i, 0, :], cnt[:, i, 2, :], ALU.add))
            m = VE.did(dve.tensor_scalar(keep[:, i, :], cnt[:, i, 1, :], NSEL + 0.5, None, ALU.is_gt))
            VE.wait(m)
            for t in range(T):
                VE.did(dve.tensor_scalar(GT[:, T * b + t, :], slots[:, :], rank[:, i, t:t + 1], None, ALU.is_equal))
                m = VE.did(dve.scalar_tensor_tensor(out=X[:, T * b + t, :], in0=X3[:, T * b + t, 0:D],
                                                    scalar=keep[:, i, t:t + 1], in1=X[:, T * b + t, :],
                                                    op0=ALU.mult, op1=ALU.add))
            sel_steps[b] = m

        def prepare(b):
            todo = [lambda t0=t0, part=part: transpose_context(b, part, t0, min(t0 + 7, KT))
                    for part in range(2) for t0 in (0, 7)]
            todo += [lambda hp=hp: make_queries(b, hp) for hp in range(HP)]
            todo += [lambda ht=ht, half=half: max_chunk(b, ht, half) for ht in range(H * T) for half in range(2)]
            return todo + [lambda: finish_max(b)]

        split_context(0)
        ctx_in[1] = load_context(1)
        split_context(1)
        for step in prepare(0):
            step()
        TOTAL = B * TILES
        START = AV_LAG + 8
        for n in range(TOTAL + AV_LAG):
            b, k = n // TILES, n % TILES
            if k == 0 and b < B:
                todo = prepare(b + 1) if b + 1 < B else []
                given = 0
            if k == 0 and 1 <= b and b + 1 < B:
                ctx_in[b + 1] = load_context(b + 1)
            if k == AV_LAG and 1 <= b and b + 1 < B:
                split_context(b + 1)
            if n < TOTAL:
                scores_tile(n)
            if n >= AV_LAG:
                v = n - AV_LAG
                values_tile(v)
            if n < TOTAL:
                want = max(0, min(len(todo), (k - START + 1) * len(todo) // (TILES - 8 - START)))
                while given < want:
                    todo[given]()
                    given += 1
            w = n - AV_LAG - 3
            for late, j in ((0, 0), (2, 1)):
                w = n - AV_LAG - 2 - late
                if w >= 0 and w % KT == KT - 1:
                    project_head(w // TILES, 2 * (w % TILES // KT) + j)
            w = n - AV_LAG - 8
            if w >= 0 and w % TILES == TILES - 1:
                select_norm(w // TILES)
                select_rank(w // TILES)
        project_head(B - 1, H - 2)
        project_head(B - 1, H - 1)
        select_norm(B - 1)
        select_rank(B - 1)

        every = [sel_steps[B - 1], small_free[0], acc_free[0], *max_free[0], *max_free[1], st_free[0], st_free[1]]
        PE.wait(*every)
        regions.pop().close()
        XS = sb("XS", [P, NG, D + 2])
        for gq in range(NG):
            for b4 in range(4):
                for t in range(T):
                    tt = (4 * gq + b4) * T + t
                    r = slice(32 * b4, 32 * b4 + 32)
                    pe.matmul(PS[r, gq, 0:D + 2], GT[:, tt, :], X3[:, tt, :], start=(t == 0), stop=(t == T - 1))
                for t in range(T):
                    tt = (4 * gq + b4) * T + t
                    r = slice(32 * b4, 32 * b4 + 32)
                    m = pe.matmul(PS[r, 4 + gq, 0:S], GT[:, tt, :], msk[:, min(4 * gq + b4, MB - 1), t, :],
                                  start=(t == 0), stop=(t == T - 1))
            gathered = PE.did(m)
            VE.wait(gathered)
            xs_ready = VE.did(dve.tensor_copy(XS[:, gq, :], PS[:, gq, 0:D + 2]))
            AC.wait(gathered)
            if gq == 0:
                mrow = sb("mrow", [P, NG, S])
            mrow_ready = AC.did(act.activation(mrow[:, gq, :], PS[:, 4 + gq, 0:S], ACT.Copy))

        ss = sb("ss", [P, 2, NG])
        hn = sb("hn", [P, NG, D])
        sq = sb("sq", [P, NG, D])

        def rmsnorm_rows(x_of, gain, which, after):
            VE.wait(after)
            for k in range(NG):
                m = VE.did(dve.tensor_tensor_reduce(out=sq[:, k, :], in0=x_of(k), in1=x_of(k), scale=1.0, scalar=0.0,
                                                    op0=ALU.mult, op1=ALU.add, accum_out=ss[:, which, k:k + 1]))
            r = rsqrt(ss[:, which, :], ss[:, which, :], NG, 1.0 / D, RMS_EPS, m)
            VE.wait(r)
            for k in range(NG):
                m = VE.did(dve.scalar_tensor_tensor(out=hn[:, k, :], in0=x_of(k), scalar=ss[:, which, k:k + 1],
                                                    in1=gain[:, :], op0=ALU.mult, op1=ALU.mult))
            return m

        def transpose_rows(dst, src_of, bank, after):
            PE.wait(*after)
            for k in range(NG):
                m = pe.transpose(PS[:, bank, k * P:(k + 1) * P], src_of(k), ident[:, :])
            m = PE.did(m)
            AC.wait(m)
            return AC.did(act.activation(dst, PS[:, bank, :], ACT.Copy))

        hn_ready = rmsnorm_rows(lambda k: XS[:, k, 0:D], ln1r, 0, xs_ready)
        hnT = sb("hnT", [P, NG * P])
        hnT_ready = transpose_rows(hnT[:, :], lambda k: hn[:, k, :], 0, (hn_ready,))

        TURN = (6.28125, 0.00193500518798828125, 3.0199159819560e-07)
        MAGIC = 1.5 * 2.0 ** 23
        PI = 3.1415925
        ang = sb("ang", [P, NG, FD // 2])
        turns = sb("turns", [P, NG, FD // 2])
        trig = sb("trig", [P, 2, NG, FD // 2])
        VE.wait(xs_ready, consts)
        m = VE.did(dve.tensor_tensor(ang[:, :, :], XS[:, :, D + 1:D + 2].to_broadcast([P, NG, FD // 2]),
                                     inv_freq[:, :].rearrange("p (o n) -> p o n", o=1).to_broadcast([P, NG, FD // 2]),
                                     ALU.mult))
        VE.wait(m)
        m = VE.did(dve.tensor_scalar(turns[:, :, :], ang[:, :, :], float(1 / (2 * np.pi)), MAGIC, ALU.mult, ALU.add))
        VE.wait(m)
        m = VE.did(dve.tensor_scalar(turns[:, :, :], turns[:, :, :], -MAGIC, None, ALU.add))
        for part in TURN:
            VE.wait(m)
            m = VE.did(dve.scalar_tensor_tensor(out=ang[:, :, :], in0=turns[:, :, :], scalar=-part, in1=ang[:, :, :],
                                                op0=ALU.mult, op1=ALU.add))
        VE.wait(m)
        m = VE.did(dve.tensor_scalar(trig[:, 0, :, :], ang[:, :, :], float(np.pi / 2), None, ALU.add))
        VE.wait(m)
        m = VE.did(dve.tensor_scalar(turns[:, :, :], trig[:, 0, :, :], PI, -2 * np.pi, ALU.is_gt, ALU.mult))
        VE.wait(m)
        m = VE.did(dve.tensor_tensor(trig[:, 0, :, :], trig[:, 0, :, :], turns[:, :, :], ALU.add))
        VE.wait(m)
        VE.did(dve.tensor_scalar(trig[:, 0, :, :], trig[:, 0, :, :], -PI, PI, ALU.max, ALU.min))
        m = VE.did(dve.tensor_scalar(trig[:, 1, :, :], ang[:, :, :], -PI, PI, ALU.max, ALU.min))
        AC.wait(m)
        trig_ready = AC.did(act.activation(trig[:, :, :, :], trig[:, :, :, :], ACT.Sin))

        mrT = sb("mrT", [P, NG, T, P])
        PE.wait(mrow_ready)
        for gq in range(NG):
            for t in range(T):
                m = pe.transpose(PS[:, 4 + gq // 2, ((gq % 2) * T + t) * P:((gq % 2) * T + t + 1) * P],
                                 mrow[:, gq, t:S:T], ident[:, :])
        m = PE.did(m)
        VE.wait(m)
        m = VE.did(dve.tensor_copy(mrT[:, :, :, :],
                                   PS[:, 4:6, :].rearrange("p k (g t q) -> p (k g) t q", t=T, q=P)))
        PE.wait(m)
        for gq in range(NG):
            for b4 in range(4):
                r = slice(32 * b4, 32 * b4 + 32)
                for t in range(T):
                    m = pe.matmul(PS[r, 6, gq * CAP:(gq + 1) * CAP], mrT[:, gq, t, 32 * b4:32 * b4 + 32],
                                  GT[:, (4 * gq + b4) * T + t, :], start=(t == 0), stop=(t == T - 1))
        m = PE.did(m)
        msel = sb("msel", [P, NG, CAP])
        VE.wait(m)
        msel_ready = VE.did(dve.tensor_copy(msel[:, :, :], PS[:, 6, 0:NG * CAP].rearrange("p (g k) -> p g k", k=CAP)))

        QK = sb("QK", [P, NG, 2, FH, 2, FD // 2])
        PE.wait(hnT_ready, fw_in, xs_ready)
        for gq in range(NG):
            m = pe.matmul(PS[:, 1 + gq // 2, (gq % 2) * S:(gq % 2 + 1) * S], hnT[:, gq * P:(gq + 1) * P],
                          fwq[:, :, :], start=True, stop=True)
        m = PE.did(m)
        AC.wait(m)
        qk_ready = AC.did(act.activation(QK[:, :, :, :, :, :].rearrange("p g w h u f -> p (g w h u f)"),
                                         PS[:, 1:3, :].rearrange("p k n -> p (k n)"), ACT.Copy))
        VX = sb("VX", [P, B, FH // 4, 32])
        vbank = (3, 4, 5, 7)
        hn4 = sb("hn4", [P, B, 4, 32])
        AC.wait(hnT_ready)
        m = AC.did(act.activation(
            hn4[:, :, :, :],
            hnT[:, :].rearrange("p (b o k) -> p b o k", o=1, k=32).to_broadcast([P, B, 4, 32]), ACT.Copy))
        PE.wait(msel_ready, m)
        for gq in range(NG):
            for b4 in range(4):
                b = 4 * gq + b4
                m = pe.matmul(PS[:, vbank[gq], b4 * P:(b4 + 1) * P],
                              hn4[:, b, :, :].rearrange("p r k -> p (r k)"),
                              fwv[:, :], start=True, stop=True)
            m = PE.did(m)
            VE.wait(m)
            vx_ready = VE.did(dve.tensor_tensor(
                VX[:, 4 * gq:4 * gq + 4, :, :].rearrange("p b h n -> p (b h) n"),
                PS[:, vbank[gq], :].rearrange("p (b n) -> p b n", n=32),
                blockmask[:, :].rearrange("p (o n) -> p o n", o=1).to_broadcast([P, FH, 32]), ALU.mult))

        QR = sb("QR", [P, NG, 2, FH, 2, FD // 2])
        rt = sb("rt", [P, 2, NG, 2 * FH, FD // 2])
        VE.wait(qk_ready, trig_ready)
        PO.wait(qk_ready, trig_ready)
        for gq in range(NG):
            src = QK[:, gq, :, :, :, :].rearrange("p w h u f -> p (w h) u f")
            dst = QR[:, gq, :, :, :, :].rearrange("p w h u f -> p (w h) u f")
            co, si = (trig[:, k, gq:gq + 1, :].to_broadcast([P, 2 * FH, FD // 2]) for k in range(2))
            VE.did(dve.tensor_tensor(dst[:, :, 0, :], src[:, :, 0, :], co, ALU.mult))
            VE.did(dve.tensor_tensor(dst[:, :, 1, :], src[:, :, 1, :], co, ALU.mult))
            VE.did(dve.tensor_tensor(rt[:, 0, gq, :, :], src[:, :, 1, :], si, ALU.mult))
            m = VE.did(dve.tensor_tensor(rt[:, 1, gq, :, :], src[:, :, 0, :], si, ALU.mult))
        VE.wait(m)
        for gq in range(NG):
            dst = QR[:, gq, :, :, :, :].rearrange("p w h u f -> p (w h) u f")
            VE.did(dve.tensor_tensor(dst[:, :, 0, :], dst[:, :, 0, :], rt[:, 0, gq, :, :], ALU.subtract))
            m = VE.did(dve.tensor_tensor(dst[:, :, 1, :], dst[:, :, 1, :], rt[:, 1, gq, :, :], ALU.add))
        rope_ready = m
        fqT = sb("fqT", [P, NG * P])
        fkT = sb("fkT", [P, NG * P])
        flat = lambda w: (lambda k: QR[:, k, w, :, :, :].rearrange("p h u f -> p (h u f)"))
        fkT_ready = transpose_rows(fkT[:, :], flat(1), 0, (rope_ready, hnT_ready))
        fqT_ready = transpose_rows(fqT[:, :], flat(0), 6, (rope_ready, msel_ready))

        KX = sb("KX", [P, 4, FH, CAP])
        SC = sb("SC", [P, NG, FH, CAP])
        zeroed = PO.did(pool.memset(SC[:, :, :, NSEL:CAP], 0.0))
        fmx = sb("fmx", [P, NG, FH])
        fden = sb("fden", [P, NG, FH])
        sbank = (1, 2, 3, 4)
        kx_used = {}
        PE.wait(fqT_ready, vx_ready, qk_ready)
        for gq in range(NG):
            for b4 in range(4):
                b = 4 * gq + b4
                VE.wait(fkT_ready, kx_used.get(b - 4))
                m = VE.did(dve.tensor_tensor(
                    KX[:, b4, :, :],
                    fkT[:, b * 32:(b + 1) * 32].rearrange("p (o k) -> p o k", o=1).to_broadcast([P, FH, CAP]),
                    headmask[:, :].rearrange("p (h o) -> p h o", o=1).to_broadcast([P, FH, CAP]), ALU.mult))
                PE.wait(m)
                m = PE.did(pe.matmul(PS[32 * b4:32 * b4 + 32, sbank[gq], :], fqT[:, b * 32:(b + 1) * 32],
                                     KX[:, b4, :, :], start=True, stop=True))
                kx_used[b] = m
            VE.wait(m, msel_ready)
            m = VE.did(dve.scalar_tensor_tensor(
                out=SC[:, gq, :, 0:NSEL],
                in0=PS[:, sbank[gq], :].rearrange("p (h k) -> p h k", k=CAP)[:, :, 0:NSEL], scalar=float(FD) ** -0.5,
                in1=msel[:, gq:gq + 1, 0:NSEL].to_broadcast([P, FH, NSEL]), op0=ALU.mult, op1=ALU.add))
            VE.wait(m)
            m = VE.did(dve.tensor_reduce(fmx[:, gq, :], SC[:, gq, :, 0:NSEL], AX_X, ALU.max))
            VE.wait(m)
            m = VE.did(dve.tensor_tensor(
                SC[:, gq, :, 0:NSEL], SC[:, gq, :, 0:NSEL],
                fmx[:, gq, :].rearrange("p (h o) -> p h o", o=1).to_broadcast([P, FH, NSEL]), ALU.subtract))
            AC.wait(m)
            e_done = AC.did(act.activation(SC[:, gq, :, 0:NSEL], SC[:, gq, :, 0:NSEL], ACT.Exp))
            VE.wait(e_done)
            m = VE.did(dve.tensor_reduce(fden[:, gq, :], SC[:, gq, :, 0:NSEL], AX_X, ALU.add))
            VE.wait(m)
            den_ready = VE.did(dve.reciprocal(fden[:, gq, :], fden[:, gq, :]))
        eT = sb("eT", [P, NG, FH // 4, P])
        tbank = (0, 5, 6, 7)
        ON = sb("ON", [P, NG, FH, FD])
        PE.wait(e_done, fkT_ready, fqT_ready, vx_ready, zeroed)
        for gq in range(NG):
            for hh in range(FH // 4):
                m = pe.transpose(PS[:, tbank[gq], hh * P:(hh + 1) * P],
                                 SC[:, gq, 4 * hh:4 * hh + 4, :].rearrange("p h k -> p (h k)"), ident[:, :])
            m = PE.did(m)
            AC.wait(m)
            et_ready = AC.did(act.activation(eT[:, gq, :, :], PS[:, tbank[gq], :].rearrange("p (h q) -> p h q", q=P),
                                             ACT.Copy))
            PE.wait(et_ready, den_ready)
            for b4 in range(4):
                for hh in range(FH // 4):
                    m = pe.matmul(PS[32 * b4:32 * b4 + 32, 1, gq * P + hh * 32:gq * P + hh * 32 + 32],
                                  eT[:, gq, hh, 32 * b4:32 * b4 + 32], VX[:, 4 * gq + b4, hh, :],
                                  start=True, stop=True)
            o_done = PE.did(m)
        VE.wait(o_done)
        m = VE.did(dve.tensor_tensor(
            ON[:, :, :, :].rearrange("p g h d -> p (g h) d"), PS[:, 1, :].rearrange("p (n d) -> p n d", d=FD),
            fden[:, :, :].rearrange("p g (h o) -> p (g h) o", o=1).to_broadcast([P, NG * FH, FD]), ALU.mult))
        oT = sb("oT", [P, NG * P])
        oT_ready = transpose_rows(oT[:, :], lambda k: ON[:, k, :, :].rearrange("p h d -> p (h d)"), 2, (m,))
        PE.wait(oT_ready)
        for gq in range(NG):
            m = pe.matmul(PS[:, 3, gq * P:(gq + 1) * P], oT[:, gq * P:(gq + 1) * P], fwo[:, :], start=True, stop=True)
        m = PE.did(m)
        XA = sb("XA", [P, NG, D])
        VE.wait(m)
        m = VE.did(dve.tensor_tensor(XA[:, :, :], PS[:, 3, :].rearrange("p (g d) -> p g d", d=D), XS[:, :, 0:D],
                                     ALU.add))
        hn2_ready = rmsnorm_rows(lambda k: XA[:, k, :], ln2r, 1, m)
        hn2T = sb("hn2T", [P, NG * P])
        hn2T_ready = transpose_rows(hn2T[:, :], lambda k: hn[:, k, :], 4, (hn2_ready,))

        GS = sb("GS", [P, NG, T, P])
        GTt = sb("GTt", [P, T, B * CAP])
        PO.wait(sel_steps[B - 1])
        for t in range(T):
            gtt = PO.did(pool.tensor_copy(GTt[:, t, :].rearrange("p (b k) -> p b k", k=CAP),
                                          GT[:, :, :].rearrange("p (b t) k -> p t b k", t=T)[:, t, :, :]))
        PE.wait(m, oT_ready, gtt)
        for gq in range(NG):
            for t in range(T):
                src = GTt[:, t, gq * P:(gq + 1) * P]
                m = pe.transpose(PS[:, 2 + gq // 2, ((gq % 2) * T + t) * P:((gq % 2) * T + t + 1) * P], src,
                                 ident[:, :])
        m = PE.did(m)
        VE.wait(m)
        gs_ready = VE.did(dve.tensor_copy(GS[:, :, :, :].rearrange("p g t n -> p (g t n)"),
                                          PS[:, 2:4, :].rearrange("p k n -> p (k n)")))

        HT = sb("HT", [P, F // P, NG * P])
        PE.wait(hn2T_ready, et_ready)
        for f in range(F // P):
            m = PE.did(pe.matmul(PS[:, tbank[f], :], fw1[:, f * P:(f + 1) * P], hn2T[:, :], start=True, stop=True))
            AC.wait(m)
            ht_ready = AC.did(act.activation(HT[:, f, :], PS[:, tbank[f], :], ACT.Gelu_apprx_tanh))
        PE.wait(ht_ready)
        for gq in range(NG):
            for f in range(F // P):
                m = pe.matmul(PS[:, 1, gq * P:(gq + 1) * P], HT[:, f, gq * P:(gq + 1) * P], fw2[:, f, :],
                              start=(f == 0), stop=(f == F // P - 1))
        m = PE.did(m)
        VE.wait(m)
        m = VE.did(dve.tensor_tensor(XA[:, :, :], PS[:, 1, :].rearrange("p (g d) -> p g d", d=D), XA[:, :, :], ALU.add))
        VE.wait(m)
        for gq in range(NG):
            m = VE.did(dve.tensor_scalar(XA[:, gq, :], XA[:, gq, :], XS[:, gq, D:D + 1], None, ALU.mult))

        PE.wait(m, gs_ready, ht_ready, hn2T_ready)
        out_dram = out.rearrange("b (p t) d -> p b t d", t=T)
        stored = Arrival(sem("stored"))
        for g2 in range(2):
            for gl in range(2):
                for t in range(T):
                    for b4 in range(4):
                        gq = 2 * g2 + gl
                        r = slice(32 * b4, 32 * b4 + 32)
                        mm = pe.matmul(PS[:, 2 * b4 + g2, (gl * T + t) * P:(gl * T + t + 1) * P], GS[r, gq, t, :],
                                       XA[r, gq, :], start=True, stop=True)
            m = PE.did(mm)
            VE.wait(m)
            for b4 in range(4):
                xv = X[:, :, :].rearrange("p (g b t) d -> p g b t d", b=4, t=T)[:, 2 * g2:2 * g2 + 2, b4, :, :]
                m = VE.did(dve.tensor_tensor(xv, PS[:, 2 * b4 + g2, :].rearrange("p (g t d) -> p g t d", g=2, t=T), xv,
                                             ALU.add))
            SP.wait(m)
            last = stored.of(sp.dma_start(out_dram[:, 8 * g2:8 * g2 + 8, :, :], X4[:, 8 * g2:8 * g2 + 8, :, :]))
        SP.wait(last)


_NAMES = {
    "x": "x", "ctx_768": "ctx_768", "w_v": "L0_attn_w_v", "b_q": "L0_attn_b_q", "b_k": "L0_attn_b_k",
    "b_v": "L0_attn_b_v", "b_out": "L0_attn_b_out", "xWo": "L0_xattn_Wo", "xbo": "L0_xattn_bo",
    "attention_mask": "L0_ffn_attention_mask", "position_ids": "L0_ffn_position_ids",
    "router_w": "L0_ffn_router_w", "router_b": "L0_ffn_router_b", "fwq": "L0_ffn_wq", "fwk": "L0_ffn_wk",
    "fwv": "L0_ffn_wv", "fwo": "L0_ffn_wo", "fw1": "L0_ffn_w1", "fw2": "L0_ffn_w2", "ln1": "L0_ffn_ln1",
    "ln2": "L0_ffn_ln2",
}
_TRANSPOSED = {
    "w_qT": "L0_attn_w_q", "w_kT": "L0_attn_w_k", "w_outT": "L0_attn_w_out", "xWqT": "L0_xattn_Wq",
    "xWkT": "L0_xattn_Wk", "xWvT": "L0_xattn_Wv",
}


def kernel(**inputs):
    import concourse.bacc as bacc
    from concourse.bass_utils import run_bass_kernel_spmd

    nc = bacc.Bacc("TRN2", target_bir_lowering=False, num_devices=1)
    arrays, aps = {}, {}
    for names, flip in ((_NAMES, False), (_TRANSPOSED, True)):
        for name, source in names.items():
            v = np.asarray(inputs[source])
            v = np.ascontiguousarray(v.T if flip else v)
            arrays[f"in_{name}"] = v
            aps[name] = nc.dram_tensor(f"in_{name}", v.shape, mybir.dt.from_np(v.dtype), kind="ExternalInput").ap()
    out = nc.dram_tensor("out_x", (B, S, D), F32, kind="ExternalOutput").ap()
    build(nc, aps, out)
    r = run_bass_kernel_spmd(nc, [arrays], core_ids=[0])
    return r.results[0]["out_x"]
```

```python
from contextlib import ExitStack

import numpy as np

import concourse.bass as bass
from concourse import mybir

F32 = mybir.dt.float32
BF16 = mybir.dt.bfloat16
I32 = mybir.dt.int32
ALU = mybir.AluOpType
ACT = mybir.ActivationFunctionType
AX_X = mybir.AxisListType.X

P = 128
B, S, D = 16, 256, 128
T = S // P
NC, DC = 1601, 96
H, DH = 16, 64
KT = 13
KP = -(-NC // KT)
KFULL = NC - (KP - 1) * KT
HP = H // 2
W2 = 2 * S
TILES = HP * KT
F = 512
FH, FD = 16, 8
CAP = S // 8
NSEL = CAP - 1
MB, MS = 4, 512
NG = B // 4
LN_EPS, RMS_EPS = 1e-5, 1e-6
ROPE_BASE = 10000.0
PRING = 8
AV_LAG = 4


class Mark:

    def __init__(self, sem, value):
        self.sem, self.value = sem, value


class Engine:

    def __init__(self, eng, sem):
        self.eng, self.sem, self.n, self.seen = eng, sem, 0, {}

    def did(self, ins):
        self.n += 1
        ins.then_inc(self.sem, 1)
        return Mark(self.sem, self.n)

    def wait(self, *marks):
        for m in marks:
            if m is not None and self.seen.get(id(m.sem), 0) < m.value:
                self.eng.wait_ge(m.sem, m.value)
                self.seen[id(m.sem)] = m.value


class Arrival:

    def __init__(self, sem):
        self.sem, self.n = sem, 0

    def of(self, dma):
        self.n += 16
        dma.then_inc(self.sem, 16)
        return Mark(self.sem, self.n)


def build(nc, a, out):
    with ExitStack() as ctx:

        regions = [ctx.enter_context(ExitStack())]

        def sb(name, shape, dt=F32):
            return regions[-1].enter_context(nc.sbuf_tensor(name, shape, dt))

        def sem(name):
            return ctx.enter_context(nc.semaphore(name))

        PE = Engine(nc.tensor, sem("pe_steps"))
        AC = Engine(nc.scalar, sem("act_steps"))
        VE = Engine(nc.vector, sem("dve_steps"))
        PO = Engine(nc.gpsimd, sem("pool_steps"))
        SP = Engine(nc.sync, sem("sp_steps"))
        pe, act, dve, pool, sp = PE.eng, AC.eng, VE.eng, PO.eng, SP.eng
        arrival = {}

        def load(key, dst, src, eng=sp):
            if key not in arrival:
                arrival[key] = Arrival(sem("in_" + key))
            return arrival[key].of(eng.dma_start(dst, src))

        PS = ctx.enter_context(nc.psum_tensor("PS", [P, 8, 512], F32))

        ident = sb("ident", [P, P])
        identb = sb("identb", [P, P], BF16)
        minus_half = sb("minus_half", [P, 8])
        lower = sb("lower", [P, T, T, P])
        slots = sb("slots", [P, CAP])
        sloti = sb("sloti", [P, CAP], I32)
        headmask = sb("headmask", [P, FH])
        blockmask = sb("blockmask", [P, 32])
        inv_freq = sb("inv_freq", [P, FD // 2])

        wqT = sb("wqT", [P, P])
        wkT = sb("wkT", [P, P])
        wv = sb("wv", [P, P])
        woutT = sb("woutT", [P, P])
        wvo = sb("wvo", [P, P])
        cols = sb("cols", [P, 3])
        brow = sb("brow", [P, P])
        xbo = sb("xbo", [P, P])
        crow = sb("crow", [P, P])
        big = {n: (n, [P, HP, D if n in ("xWqT", "xWo") else DC]) for n in ("xWqT", "xWkT", "xWvT", "xWo")}
        fwq = sb("fwq", [P, 2, P])
        fwv = sb("fwv", [P, P])
        fwo = sb("fwo", [P, P])
        fw1 = sb("fw1", [P, F])
        fw2 = sb("fw2", [P, F // P, P])
        ln1r = sb("ln1r", [P, P])
        ln2r = sb("ln2r", [P, P])
        rwr = sb("rwr", [P, P])
        rbc = sb("rbc", [P, 1])
        posi = sb("posi", [P, MB, T], I32)
        msk = sb("msk", [P, MB, T, S])

        X = sb("X", [P, B * T, D])
        X3 = sb("X3", [P, B * T, D + 2])
        GT = sb("GT", [P, B * T, CAP])

        x_dram = a["x"].rearrange("b (p t) d -> p b t d", t=T)
        X4 = X[:, :, :].rearrange("p (b t) d -> p b t d", t=T)
        x_in = []
        for b in range(B):
            x_in.append(load(f"x{b}", X4[:, b, :, :], x_dram[:, b, :, :]))
            if b == 0:
                for n, t in (("w_qT", wqT), ("w_kT", wkT), ("w_v", wv), ("w_outT", woutT)):
                    w_in = load("w", t[:, :], a[n], act)
                for i, n in enumerate(("b_q", "b_k", "b_v")):
                    w_in = load("w", cols[:, i:i + 1], a[n].rearrange("(p o) -> p o", o=1), act)
                for n, t in (("b_out", brow), ("xbo", xbo), ("ln1", ln1r), ("ln2", ln2r)):
                    w_in = load("w", t[:, :], a[n].rearrange("(o n) -> o n", o=1).to_broadcast([P, P]), act)
                w_in = load("w", rwr[:, :], a["router_w"].rearrange("n o -> o n").to_broadcast([P, P]), act)
                w_in = load("w", rbc[:, :], a["router_b"].rearrange("(o n) -> o n", o=1).to_broadcast([P, 1]), act)
        stats = sb("stats", [P, 3, T, 6])
        mv = sb("mv", [P, 3, T, 2])
        rstd = sb("rstd", [P, 3, T])
        junk = sb("junk", [P, 8, S], BF16)
        cnt = sb("cnt", [P, 2, 3, T])
        wraw = sb("wraw", [P, 2, T])
        keep = sb("keep", [P, 2, T])
        rank = sb("rank", [P, 2, T])

        regions.append(ctx.enter_context(ExitStack()))
        X2T = sb("X2T", [P, 2, B, S], BF16)
        G = sb("G", [P, 2, H, DC], BF16)
        M = sb("M", [DC + 1, H, D + 1])
        rxa = sb("rxa", [P, 2, T])
        Cf = sb("Cf", [KP, KT, DC])
        Ch = [sb(f"Ch{i}", [KP, KT, DC + 1], BF16) for i in range(2)]
        Cl = [sb(f"Cl{i}", [KP, KT, DC], BF16) for i in range(2)]
        ChT = [sb(f"ChT{i}", [DC + 2, KT, KP], BF16) for i in range(2)]
        ClT = [sb(f"ClT{i}", [DC, KT, KP], BF16) for i in range(2)]
        AH = [sb(f"AH{i}", [DC + 2, H * S], BF16) for i in range(2)]
        AL = [sb(f"AL{i}", [DC, H * S], BF16) for i in range(2)]
        U = [sb(f"U{i}", [DC + 1, W2]) for i in range(2)]
        pmax = sb("pmax", [P, 2, H * T, 2])
        nmax = sb("nmax", [P, 2, H * T])
        mh = sb("mh", [H * T, P], BF16)
        ml = sb("ml", [H * T, P], BF16)

        xn = sb("xn", [P, T, D])
        xT = sb("xT", [P, S])
        qT = sb("qT", [P, S])
        kT = sb("kT", [P, S])
        vp = sb("vp", [P, T, D])
        nm = sb("nm", [P, T])
        den = sb("den", [P, T])
        rden = sb("rden", [P, T])
        ex = sb("ex", [P, T, S])
        exT = sb("exT", [P, T, T, P])
        xn2 = sb("xn2", [P, T, D])
        regions.append(ctx.enter_context(ExitStack()))
        big = {n: sb(*v) for n, v in big.items()}
        for n in big:
            big_in = load("xw", big[n][:, :, :], a[n].rearrange("(j p) n -> p j n", p=P), act)

        def load_context(b):
            c = a["ctx_768"]
            last = (KP - 1) * KT
            sp_wait = (c_split.get(b - 1),)
            SP.wait(*sp_wait)
            load("ctx", Cf[0:KP - 1, :, :], c[b, 0:last, :].rearrange("(p t) d -> p t d", t=KT))
            load("ctx", Cf[KP - 1:KP, 0:KFULL, :],
                 c[b, last:NC, :].rearrange("(o t) d -> o t d", o=1))
            return load("ctx", Cf[KP - 1:KP, KFULL:KT, :],
                        c[b, NC - (KT - KFULL):NC, :].rearrange("(o t) d -> o t d", o=1))

        c_split = {}
        ctx_in = {0: load_context(0)}
        for n, t in (("wq", fwq[:, 0, :]), ("wk", fwq[:, 1, :]), ("wv", fwv[:, :]), ("wo", fwo[:, :]),
                     ("w1", fw1[:, :]), ("w2", fw2[:, :, :])):
            src = a["f" + n]
            fw_in = load("fw", t, src.rearrange("(j p) n -> p j n", p=P) if n == "w2" else src)
        fw_in = load("fw", posi[:, :, :], a["position_ids"][:, 0:S].rearrange("b (p t) -> p b t", t=T))
        for mb in range(MB):
            fw_in = load("fw", msk[:, mb, :, :],
                         a["attention_mask"][mb, 0, 0:S, 0:S].rearrange("(p t) n -> p t n", t=T))

        def const(ins):
            m = PO.did(ins)
            PO.wait(m)
            return m

        const(pool.memset(ident[:, :], 0.0))
        const(pool.memset(identb[:, :], 0.0))
        const(pool.memset(lower[:, :, :, :], 1.0))
        m0 = const(pool.memset(headmask[:, :], 1.0))
        m0 = const(pool.memset(blockmask[:, :], 1.0))
        PO.wait(m0)
        for t in (ident, identb):
            ident_ready = const(pool.affine_select(out=t[:, :], in_=t[:, :], compare_op=ALU.not_equal, fill=1.0,
                                                    base=0, pattern=[[-1, P]], channel_multiplier=1))
        consts = const(pool.memset(minus_half[:, :], -0.5))
        for i in range(FD // 2):
            inv = float(np.float32(1.0) / np.power(np.float32(ROPE_BASE), np.float32(2 * i / FD)))
            const(pool.memset(inv_freq[:, i:i + 1], inv))
        for t in range(T):
            const(pool.affine_select(out=lower[:, t, :, :], in_=lower[:, t, :, :], compare_op=ALU.is_gt, fill=0.0,
                                      base=t, pattern=[[-1, T], [-T, P]], channel_multiplier=T))
        m1 = const(pool.affine_select(out=headmask[:, :], in_=headmask[:, :], compare_op=ALU.is_ge, fill=0.0,
                                       base=0, pattern=[[-FD, FH]], channel_multiplier=1))
        m2 = const(pool.affine_select(out=blockmask[:, :].rearrange("p (h d) -> p h d", d=FD),
                                       in_=blockmask[:, :].rearrange("p (h d) -> p h d", d=FD),
                                       compare_op=ALU.is_ge, fill=0.0,
                                       base=0, pattern=[[-32, 4], [0, FD]], channel_multiplier=1))
        PO.wait(m1, m2)
        const(pool.affine_select(out=headmask[:, :], in_=headmask[:, :], compare_op=ALU.is_ge, fill=0.0,
                                  base=FD - 1, pattern=[[FD, FH]], channel_multiplier=-1))
        const(pool.affine_select(out=blockmask[:, :].rearrange("p (h d) -> p h d", d=FD),
                                  in_=blockmask[:, :].rearrange("p (h d) -> p h d", d=FD),
                                  compare_op=ALU.is_ge, fill=0.0,
                                  base=31, pattern=[[32, 4], [0, FD]], channel_multiplier=-1))
        m3 = const(pool.iota(sloti[:, :], pattern=[[1, CAP]], base=0, channel_multiplier=0))
        PO.wait(m3)
        m4 = const(pool.tensor_copy(slots[:, :], sloti[:, :]))
        PO.wait(m4)
        const(pool.memset(slots[:, NSEL:CAP], -1.0))
        for i in range(2):
            const(pool.memset(ChT[i][DC:DC + 2, :, :], 1.0))
            const(pool.memset(Ch[i][:, :, DC:DC + 1], 1.0))
        const(pool.memset(M[:, :, :], 0.0))
        consts = const(pool.memset(M[DC:DC + 1, :, D:D + 1], 1.0))

        def rsqrt(dst, var, n, scale, eps, after):
            PO.wait(after)
            m = PO.did(pool.tensor_scalar(dst, var, scale, eps, ALU.mult, ALU.add))
            PO.wait(m)
            return PO.did(pool.tensor_tensor(dst, dst, minus_half[:, 0:n], ALU.pow))

        PE.wait(w_in, ident_ready)
        pe.matmul(PS[:, 0, 0:P], wv[:, :], woutT[:, :], start=True, stop=True)
        made = PE.did(pe.matmul(PS[:, 1, 0:P], cols[:, 2:3].to_broadcast([P, P]), woutT[:, :], start=True, stop=True))
        VE.wait(made, w_in)
        VE.did(dve.tensor_copy(wvo[:, :], PS[:, 0, 0:P]))
        wvo_ready = VE.did(dve.tensor_tensor(crow[:, :], PS[:, 1, 0:P], brow[:, :], ALU.add))
        PE.wait(big_in, wvo_ready)
        G2 = G[:, :, :, :].rearrange("p w (j e) c -> p w e j c", e=2)
        M2 = M[:, :, :].rearrange("p (j e) c -> p e j c", e=2)
        for q in range(2):
            banks = ((2, 3, 4, 5), (6, 7, 0, 1))[q]
            for even in range(2):
                r = slice(DH * even, DH * even + DH)
                for j in range(4):
                    c = j * P
                    pe.matmul(PS[:, banks[even], c:c + DC], big["xWqT"][r, 4 * q + j, :], big["xWkT"][r, 4 * q + j, :],
                              start=True, stop=True)
                    mm = pe.matmul(PS[0:DC, banks[2 + even], c:c + D], big["xWvT"][r, 4 * q + j, :],
                                   big["xWo"][r, 4 * q + j, :], start=True, stop=True)
            made = PE.did(mm)
            AC.wait(made, consts)
            VE.wait(made, consts)
            for even in range(2):
                g4 = PS[:, banks[even], :].rearrange("p (h c) -> p h c", c=P)[:, :, 0:DC]
                m4_ = PS[0:DC, banks[2 + even], :].rearrange("p (h c) -> p h c", c=P)
                js = slice(4 * q, 4 * q + 4)
                g_hi = AC.did(act.activation(G2[:, 0, even, js, :], g4, ACT.Copy, scale=DH ** -0.5))
                VE.wait(g_hi)
                VE.did(dve.scalar_tensor_tensor(out=G2[:, 1, even, js, :], in0=g4, scalar=DH ** -0.5,
                                                in1=G2[:, 0, even, js, :], op0=ALU.mult, op1=ALU.subtract))
                weights_done = VE.did(dve.tensor_copy(M2[0:DC, even, js, 0:D], m4_))

        ln_last = {}

        def norm_stats(which, b, x_mark):
            VE.wait(x_mark, ln_last.get(which))
            for t in range(T):
                m = VE.did(dve.bn_stats(stats[:, which, t, :], X[:, T * b + t, :]))
            VE.wait(m)
            for t in range(T):
                m = VE.did(dve.bn_aggr(mv[:, which, t, :], stats[:, which, t, :]))
            ln_last["rstd", which] = rsqrt(rstd[:, which, :], mv[:, which, :, 1], T, 1.0, LN_EPS, m)

        def norm_apply(which, b, dst_of, dst_free=None):
            VE.wait(ln_last["rstd", which], dst_free)
            for t in range(T):
                m = VE.did(dve.tensor_scalar(dst_of(t), X[:, T * b + t, :], mv[:, which, t, 0:1],
                                             rstd[:, which, t:t + 1], ALU.subtract, ALU.mult))
            ln_last[which] = m
            return m

        small_free = [weights_done]
        SA_SCALE = float(D) ** -0.5
        sa = {}
        bo_added, x2T_ready = {}, {}

        def sa_transpose(b):
            PE.wait(sa["xn"], ident_ready, small_free[0])
            for t in range(T):
                m = pe.transpose(PS[:, 7, t * P:(t + 1) * P], xn[:, t, :], ident[:, :])
            sa["xn_read"] = PE.did(m)
            AC.wait(sa["xn_read"], sa.get("xT_read"))
            small_free[0] = sa["xT"] = AC.did(act.activation(xT[:, :], PS[:, 7, 0:S], ACT.Copy))

        def sa_query_key(b):
            PE.wait(sa["xT"], w_in, small_free[0])
            pe.matmul(PS[:, 7, 0:S], wqT[:, :], xT[:, :], start=True, stop=True)
            m = PE.did(pe.matmul(PS[:, 7, S:2 * S], wkT[:, :], xT[:, :], start=True, stop=True))
            VE.wait(m, sa.get("scores"))
            q = VE.did(dve.tensor_scalar(qT[:, :], PS[:, 7, 0:S], cols[:, 0:1], SA_SCALE, ALU.add, ALU.mult))
            AC.wait(m, q, sa.get("scores"))
            small_free[0] = sa["qk"] = AC.did(act.activation(kT[:, :], PS[:, 7, S:2 * S], ACT.Identity,
                                                             bias=cols[:, 1:2]))

        def sa_value(b):
            PE.wait(wvo_ready, small_free[0])
            for t in range(T):
                m = pe.matmul(PS[:, 7, t * P:(t + 1) * P], xT[:, t * P:(t + 1) * P], wvo[:, :], start=True, stop=True)
            sa["xT_read"] = PE.did(m)
            AC.wait(sa["xT_read"], sa.get("out"))
            small_free[0] = sa["v"] = AC.did(act.activation(vp[:, :, :], PS[:, 7, 0:T * D].rearrange(
                "p (t d) -> p t d", d=D), ACT.Copy))

        def sa_scores(b):
            PE.wait(sa["qk"], small_free[0])
            for t in range(T):
                m = pe.matmul(PS[:, 7, t * S:(t + 1) * S], qT[:, t * P:(t + 1) * P], kT[:, :], start=True, stop=True)
            sa["scores"] = PE.did(m)
            VE.wait(sa["scores"], sa.get("ex"))
            m = VE.did(dve.tensor_reduce(nm[:, :], PS[:, 7, :].rearrange("p (t n) -> p t n", n=S), AX_X, ALU.max,
                                         negate=True))
            AC.wait(m, sa.get("ex_read"), sa.get("x1"))
            for t in range(T):
                m = AC.did(act.activation(ex[:, t, :], PS[:, 7, t * S:(t + 1) * S], ACT.Exp,
                                          bias=nm[:, t:t + 1], accum_out=den[:, t:t + 1]))
            small_free[0] = sa["ex"] = m

        def sa_turn(b):
            PE.wait(sa["ex"], small_free[0])
            for kt in range(T):
                for t in range(T):
                    c = (kt * T + t) * P
                    m = pe.transpose(PS[:, 7, c:c + P], ex[:, t, kt * P:(kt + 1) * P], ident[:, :])
            sa["ex_read"] = PE.did(m)
            AC.wait(sa["ex_read"], sa.get("out"))
            small_free[0] = sa["exT"] = AC.did(act.activation(
                exT[:, :, :, :], PS[:, 7, :].rearrange("p (k t q) -> p k t q", k=T, t=T), ACT.Copy))
            PO.wait(sa["xn"], wvo_ready)
            for t in range(T):
                m = PO.did(pool.tensor_tensor(X[:, T * b + t, :], X[:, T * b + t, :], crow[:, :], ALU.add))
            sa["x+c"] = m

        def sa_output(b):
            PE.wait(sa["exT"], sa["v"], small_free[0])
            for t in range(T):
                for kt in range(T):
                    m = pe.matmul(PS[:, 7, t * P:(t + 1) * P], exT[:, kt, t, :], vp[:, kt, :],
                                  start=(kt == 0), stop=(kt == T - 1))
            sa["out"] = PE.did(m)
            VE.wait(sa["ex"])
            r = VE.did(dve.reciprocal(rden[:, :], den[:, :]))
            VE.wait(sa["out"], sa["x+c"], r)
            for t in range(T):
                m = VE.did(dve.scalar_tensor_tensor(out=X[:, T * b + t, :], in0=PS[:, 7, t * P:(t + 1) * P],
                                                    scalar=rden[:, t:t + 1], in1=X[:, T * b + t, :],
                                                    op0=ALU.mult, op1=ALU.add))
            small_free[0] = sa["x1"] = m

        def sa_norm2(b):
            sa["xn2"] = m = norm_apply(1, b, lambda t: xn2[:, t, :], sa.get("xn2_read"))
            PO.wait(m)
            for t in range(T):
                bo_added[b] = PO.did(pool.tensor_tensor(X[:, T * b + t, :], X[:, T * b + t, :], xbo[:, :], ALU.add))

        def sa_finish(b):
            PE.wait(sa["xn2"], small_free[0])
            for t in range(T):
                m = pe.transpose(PS[:, 7, t * P:(t + 1) * P], xn2[:, t, :], ident[:, :])
            sa["xn2_read"] = PE.did(m)
            AC.wait(sa["xn2_read"])
            m = AC.did(act.activation(X2T[:, 0, b, :], PS[:, 7, 0:S], ACT.Copy))
            VE.wait(m)
            small_free[0] = x2T_ready[b] = VE.did(dve.tensor_tensor(X2T[:, 1, b, :], PS[:, 7, 0:S], X2T[:, 0, b, :],
                                                                    ALU.subtract))

        def self_attention(b):
            def first_norm():
                sa["xn"] = norm_apply(0, b, lambda t: xn[:, t, :], sa.get("xn_read"))

            return [lambda: norm_stats(0, b, x_in[b]), first_norm] + [
                lambda f=f: f(b) for f in (sa_transpose, sa_query_key, sa_value, sa_scores, sa_turn, sa_output)
            ] + [lambda: norm_stats(1, b, sa["x1"]), lambda: sa_norm2(b), lambda: sa_finish(b)]

        regions.pop().close()
        PF = sb("PF", [KP, PRING, W2])
        PL = sb("PL", [KP, PRING, W2], BF16)
        PH = PF[:, :, :].bitcast(BF16).rearrange("p r (n w) -> p r n w", w=2)[:, :, :, 1]
        MAXB = {0: 0, 1: 2}
        NQ = 4
        NKEY = KT * KP // NQ
        max_free = {0: weights_done, 1: weights_done}
        st_free = {0: weights_done, 1: weights_done}
        acc_free = [weights_done]
        av_done, exp_done, lo_done = {}, {}, {}
        u_free = {0: None, 1: None}
        max_used, st_used, av_used = {}, {}, {}
        x_marks = {}

        def split_context(b):
            i = b % 2
            PO.wait(ctx_in[b], av_used.get(b - 2), c_tr.get(b - 2))
            m = PO.did(pool.tensor_copy(Ch[i][:, :, 0:DC], Cf[:, :, :]))
            PO.wait(m)
            c_split[b] = PO.did(pool.tensor_tensor(Cl[i][:, :, :], Cf[:, :, :], Ch[i][:, :, 0:DC], ALU.subtract))

        c_tr, c_ready = {}, {}

        def transpose_context(b, part, t0, t1):
            i = b % 2
            src, dst = (Ch, ChT) if part == 0 else (Cl, ClT)
            bank = PS[0:DC, 7, :].bitcast(BF16)
            PE.wait(c_split[b], small_free[0], ident_ready)
            for t in range(t0, t1):
                m = pe.transpose(bank[:, (t - t0) * KP:(t - t0 + 1) * KP], src[i][:, t, 0:DC], identb[0:KP, 0:KP])
            c_tr[b] = PE.did(m)
            AC.wait(c_tr[b], st_used.get(b - 2), consts)
            m = AC.did(act.activation(dst[i][0:DC, t0:t1, :],
                                      bank[:, 0:(t1 - t0) * KP].rearrange("p (t k) -> p t k", k=KP), ACT.Copy))
            small_free[0] = c_ready[b] = m

        a_ready = {}

        def make_queries(b, hp):
            i = b % 2
            PE.wait(x2T_ready[b], small_free[0], weights_done)
            for j in range(2):
                for n, (w, x) in enumerate(((0, 0), (0, 1), (1, 0))):
                    m = pe.matmul(PS[0:DC, 7, j * S:(j + 1) * S], G[:, w, 2 * hp + j, :], X2T[:, x, b, :],
                                  start=(n == 0), stop=(n == 2))
            m = PE.did(m)
            cols_ = slice(hp * W2, (hp + 1) * W2)
            AC.wait(m, st_used.get(b - 2))
            hi = AC.did(act.activation(AH[i][0:DC, cols_], PS[0:DC, 7, :], ACT.Copy))
            VE.wait(hi)
            m = VE.did(dve.tensor_tensor(AL[i][:, cols_], PS[0:DC, 7, :], AH[i][0:DC, cols_], ALU.subtract))
            small_free[0] = a_ready[(b, hp)] = m

        def max_chunk(b, ht, half):
            i, k = b % 2, (2 * ht + half) % 2
            PE.wait(c_ready[b], a_ready[(b, ht // 4)], max_free[k])
            keys = ChT[i][0:DC, :, :].rearrange("p t k -> p (t k)")
            for n in range(2):
                c = (2 * half + n) * NKEY
                m = pe.matmul(PS[:, MAXB[k] + n, 0:NKEY], AH[i][0:DC, ht * P:(ht + 1) * P], keys[:, c:c + NKEY],
                              start=True, stop=True)
            m = PE.did(m)
            max_used[b] = m
            VE.wait(m)
            m = VE.did(dve.tensor_reduce(pmax[:, i, ht, half:half + 1], PS[:, MAXB[k]:MAXB[k] + 2, 0:NKEY],
                                         mybir.AxisListType.XY, ALU.max))
            max_free[k] = m
            pmax_done[b] = m

        m_in, m_last, nmax_done, pmax_done = {}, [None], {}, {}

        def reduce_max(b, h0, h1):
            i = b % 2
            VE.wait(pmax_done[b])
            nmax_done[b] = VE.did(dve.tensor_reduce(nmax[:, i, T * h0:T * h1], pmax[:, i, T * h0:T * h1, :], AX_X,
                                                    ALU.max, negate=True))

        def place_max(b, h0, h1):
            i, n = b % 2, T * (h1 - h0)
            PE.wait(nmax_done[b], small_free[0])
            m = PE.did(pe.transpose(PS[0:n, 7, 0:P], nmax[:, i, T * h0:T * h1], ident[:, :]))
            AC.wait(m, m_last[0])
            hi = AC.did(act.activation(mh[0:n, :], PS[0:n, 7, 0:P], ACT.Copy))
            VE.wait(hi, m_last[0])
            lo = VE.did(dve.tensor_tensor(ml[0:n, :], PS[0:n, 7, 0:P], mh[0:n, :], ALU.subtract))
            small_free[0] = lo
            SP.wait(hi, lo, st_used.get(b - 2))
            load("negmax", AH[i][DC:DC + 1, h0 * S:h1 * S], mh[0:n, :])
            m_last[0] = load("negmax", AH[i][DC + 1:DC + 2, h0 * S:h1 * S], ml[0:n, :])
            for hp in range(h0 // 2, h1 // 2):
                m_in[b, hp] = m_last[0]

        def scores_tile(n):
            b, hp, t = n // TILES, n % TILES // KT, n % KT
            i, k, r = b % 2, n % 2, n % PRING
            cols_ = slice(hp * W2, (hp + 1) * W2)
            PE.wait(m_in[b, hp], a_ready[(b, hp)], c_ready[b], st_free[k])
            o = PS[0:KP, 4 + k, :]
            pe.matmul(o, ChT[i][:, t, :], AH[i][:, cols_], start=True, stop=False)
            pe.matmul(o, ChT[i][0:DC, t, :], AL[i][:, cols_], start=False, stop=False)
            m = PE.did(pe.matmul(o, ClT[i][:, t, :], AH[i][0:DC, cols_], start=False, stop=True))
            st_used[b] = m
            AC.wait(m, av_done.get(n - PRING))
            exp_done[n] = st_free[k] = AC.did(act.activation(PF[:, r, :], o, ACT.Exp))
            if n % 2:
                VE.wait(exp_done[n], av_done.get(n - PRING))
                lo_done[n] = lo_done[n - 1] = VE.did(dve.tensor_tensor(
                    PL[:, r - 1:r + 1, :], PF[:, r - 1:r + 1, :], PH[:, r - 1:r + 1, :], ALU.subtract))

        def values_tile(n):
            b, hp, t = n // TILES, n % TILES // KT, n % KT
            i, r = b % 2, n % PRING
            rows = KP if t < KFULL else KP - 1
            PE.wait(exp_done[n], c_split[b])
            if t == 0:
                PE.wait(acc_free[0])
            c_hi, c_lo = Ch[i][0:rows, t, :], Cl[i][0:rows, t, :]
            pe.matmul(PS[0:DC + 1, 6, :], c_hi, PH[0:rows, r, :], start=(t == 0), stop=False)
            pe.matmul(PS[0:DC, 6, :], c_lo, PH[0:rows, r, :], start=False, stop=False)
            PE.wait(lo_done[n])
            m = PE.did(pe.matmul(PS[0:DC + 1, 6, :], c_hi, PL[0:rows, r, :], start=False, stop=(t == KT - 1)))
            av_done[n] = av_used[b] = m
            if t == KT - 1:
                k = (b * HP + hp) % 2
                AC.wait(m, u_free[k])
                acc_free[0] = u_ready[(b, hp)] = AC.did(act.activation(U[k][:, :], PS[0:DC + 1, 6, :], ACT.Copy))

        u_ready, x2_ready = {}, {}

        def project_head(b, h):
            k = (b * HP + h // 2) % 2
            PE.wait(u_ready[(b, h // 2)], small_free[0], weights_done)
            for t in range(T):
                c = (h % 2) * S + t * P
                m = pe.matmul(PS[:, 7, t * (D + 1):(t + 1) * (D + 1)], U[k][:, c:c + P], M[:, h, :],
                              start=True, stop=True)
            m = PE.did(m)
            u_free[k] = m
            o = PS[:, 7, 0:T * (D + 1)].rearrange("p (t n) -> p t n", n=D + 1)
            VE.wait(m, x_marks.get(("acc", h % 2)))
            m = VE.did(dve.reciprocal(rxa[:, h % 2, :], o[:, :, D]))
            VE.wait(m, x_marks.get("acc"), bo_added[b])
            for t in range(T):
                m = VE.did(dve.scalar_tensor_tensor(out=X[:, T * b + t, :], in0=o[:, t, 0:D],
                                                    scalar=rxa[:, h % 2, t:t + 1], in1=X[:, T * b + t, :],
                                                    op0=ALU.mult, op1=ALU.add))
            small_free[0] = x_marks["acc"] = x_marks[("acc", h % 2)] = x2_ready[b] = m

        sel_steps = {}

        def select_weights(b):
            m = norm_apply(2, b, lambda t: X3[:, T * b + t, 0:D])
            VE.wait(m, w_in, fw_in)
            for t in range(T):
                m = VE.did(dve.tensor_tensor_reduce(out=junk[:, 6 + t, 0:D], in0=X3[:, T * b + t, 0:D], in1=rwr[:, :],
                                                    scale=1.0, scalar=0.0, op0=ALU.mult, op1=ALU.add,
                                                    accum_out=wraw[:, b % 2, t:t + 1]))
            VE.wait(m)
            VE.did(dve.tensor_copy(X3[:, T * b:T * b + T, D + 1], posi[:, min(b, MB - 1), :]))
            sel_steps["w"] = VE.did(dve.tensor_scalar(X3[:, T * b:T * b + T, D], wraw[:, b % 2, :], rbc[:, 0:1], None,
                                                      ALU.add))

        def select_row(b):
            PE.wait(sel_steps["w"], small_free[0])
            for t in range(T):
                m = pe.transpose(PS[:, 7, t * P:(t + 1) * P], X3[:, T * b + t, D:D + 1].to_broadcast([P, P]),
                                 ident[:, :])
            sel_steps["row"] = PE.did(m)

        def select_rank(b):
            i = b % 2
            row = PS[:, 7, 0:S]
            VE.wait(sel_steps["row"], consts)
            for t in range(T):
                w = X3[:, T * b + t, D:D + 1]
                for j, op in enumerate((ALU.is_gt, ALU.is_ge)):
                    VE.did(dve.tensor_scalar(junk[:, 2 * t + j, :], row, w, None, op, ALU.add,
                                             accum_out=cnt[:, i, j, t:t + 1]))
                m = VE.did(dve.scalar_tensor_tensor(out=junk[:, 4 + t, :], in0=row, scalar=w,
                                                    in1=lower[:, t, :, :].rearrange("p u q -> p (u q)"),
                                                    op0=ALU.is_equal, op1=ALU.mult, accum_out=cnt[:, i, 2, t:t + 1]))
            small_free[0] = m
            VE.wait(m)
            VE.did(dve.tensor_tensor(rank[:, i, :], cnt[:, i, 0, :], cnt[:, i, 2, :], ALU.add))
            m = VE.did(dve.tensor_scalar(keep[:, i, :], cnt[:, i, 1, :], NSEL + 0.5, None, ALU.is_gt))
            VE.wait(m)
            for t in range(T):
                VE.did(dve.tensor_scalar(GT[:, T * b + t, :], slots[:, :], rank[:, i, t:t + 1], None, ALU.is_equal))
                m = VE.did(dve.scalar_tensor_tensor(out=X[:, T * b + t, :], in0=X3[:, T * b + t, 0:D],
                                                    scalar=keep[:, i, t:t + 1], in1=X[:, T * b + t, :],
                                                    op0=ALU.mult, op1=ALU.add))
            sel_steps[b] = m

        def maxima(b, h0, h1):
            return [lambda ht=ht, half=half: max_chunk(b, ht, half) for ht in range(T * h0, T * h1)
                    for half in range(2)] + [lambda: reduce_max(b, h0, h1), lambda: place_max(b, h0, h1)]

        def transposes_of(b):
            return [lambda t0=t0, part=part: transpose_context(b, part, t0, min(t0 + 7, KT))
                    for part in range(2) for t0 in (0, 7)]

        def queries_of(b, first, last):
            return [lambda hp=hp: make_queries(b, hp) for hp in range(first, last)]

        def spread(steps, first, last):
            return [(first + k * (last - first + 1) // len(steps), step) for k, step in enumerate(steps)]

        def chunks(b, h0, h1):
            return maxima(b, h0, h1)[:-2]

        PLACES = [k for k in range(AV_LAG + 6, TILES) if (k - AV_LAG) % KT in (6, 8, 10, 12)]
        LAST = TILES - 4

        def plan(b):
            p, n = PLACES, b + 1
            todo = []
            if b >= 1:
                after = AV_LAG + 5
                todo += [(after, lambda: norm_stats(2, b - 1, x2_ready[b - 1])),
                         (after + 2, lambda: select_weights(b - 1)), (p[4], lambda: select_row(b - 1)),
                         (p[4] + 1, lambda: select_rank(b - 1))]
            if n < B and b >= 1:
                tr, qu = transposes_of(n), queries_of(n, 0, HP)
                places = (p[0], p[1], p[5], p[6])
                todo += list(zip(places, tr))
                todo += list(zip((p[2], p[3], p[7], p[11], p[15], p[16], p[18], p[19]), qu))
                todo += spread(chunks(n, 0, H), p[2] + 1, LAST - 4)
                sa_places = (p[8], p[9], p[10], p[12], p[13], p[14], p[17])
            if b == 0:
                todo += list(zip((0, 2, 4, 6, 8, 10), queries_of(0, 2, HP)))
                for q in range(1, 4):
                    h = q * EARLY
                    end = 2 * KT * q - 7 if q == 1 else (p[9], p[12])[q - 2] - 1
                    todo += spread(chunks(0, h, h + EARLY), (2, 20, 37)[q - 1], end - 1)
                    todo += [(end, lambda h=h: reduce_max(0, h, h + EARLY)),
                             (end + 1, lambda h=h: place_max(0, h, h + EARLY))]
                todo += list(zip((p[1], p[2], p[3], p[4]), transposes_of(1)))
                todo += list(zip((p[5], p[6], p[7], p[8], p[10], p[11], p[13], p[14]), queries_of(1, 0, HP)))
                todo += spread(chunks(1, 0, H), 53, LAST - 3)
                sa_places = (p[15], p[16], p[17], p[18], p[19], p[20], p[23])
            if n < B:
                todo += [(LAST - 2, lambda: reduce_max(n, 0, H)), (LAST, lambda: place_max(n, 0, H))]
            if b + 2 < B:
                s = self_attention(b + 2)
                q = sa_places
                tiles = (q[0] - 6, q[0] - 3, *q[:6], q[5] + 2, q[5] + 5, q[6])
                todo += list(zip(tiles, s))
            return sorted(todo, key=lambda x: x[0])

        EARLY = 4
        split_context(0)
        ctx_in[1] = load_context(1)
        split_context(1)
        first = self_attention(0)
        for k, step in enumerate(first):
            step()
            if k >= len(first) - 4:
                transposes_of(0)[k - len(first) + 4]()
        for step in queries_of(0, 0, 2):
            step()
        beside = self_attention(1)
        for k, step in enumerate(chunks(0, 0, EARLY)):
            step()
            if k < len(beside):
                beside[k]()
        reduce_max(0, 0, EARLY)
        place_max(0, 0, EARLY)
        TOTAL = B * TILES
        for n in range(TOTAL + AV_LAG):
            b, k = n // TILES, n % TILES
            if k == 0 and b < B:
                todo = plan(b)
                if 1 <= b and b + 1 < B:
                    ctx_in[b + 1] = load_context(b + 1)
            if k == AV_LAG and 1 <= b and b + 1 < B:
                split_context(b + 1)
            if n < TOTAL:
                scores_tile(n)
            if n >= AV_LAG:
                values_tile(n - AV_LAG)
            while todo and todo[0][0] <= k and b < B:
                todo.pop(0)[1]()
            done = n - AV_LAG - (KT - 1)
            for late, j in ((2, 0), (4, 1)):
                if done >= late and (done - late) % KT == 0:
                    w = (done - late) // KT
                    project_head(w // HP, 2 * (w % HP) + j)
        project_head(B - 1, H - 2)
        project_head(B - 1, H - 1)
        norm_stats(2, B - 1, x2_ready[B - 1])
        select_weights(B - 1)
        select_row(B - 1)
        select_rank(B - 1)

        every = [sel_steps[B - 1], small_free[0], acc_free[0], max_free[0], max_free[1], st_free[0], st_free[1]]
        PE.wait(*every)
        regions.pop().close()
        XS = sb("XS", [P, NG, D + 2])
        for gq in range(NG):
            for b4 in range(4):
                for t in range(T):
                    tt = (4 * gq + b4) * T + t
                    r = slice(32 * b4, 32 * b4 + 32)
                    pe.matmul(PS[r, gq, 0:D + 2], GT[:, tt, :], X3[:, tt, :], start=(t == 0), stop=(t == T - 1))
                for t in range(T):
                    tt = (4 * gq + b4) * T + t
                    r = slice(32 * b4, 32 * b4 + 32)
                    m = pe.matmul(PS[r, 4 + gq, 0:S], GT[:, tt, :], msk[:, min(4 * gq + b4, MB - 1), t, :],
                                  start=(t == 0), stop=(t == T - 1))
            gathered = PE.did(m)
            VE.wait(gathered)
            xs_ready = VE.did(dve.tensor_copy(XS[:, gq, :], PS[:, gq, 0:D + 2]))
            AC.wait(gathered)
            if gq == 0:
                mrow = sb("mrow", [P, NG, S])
            mrow_ready = AC.did(act.activation(mrow[:, gq, :], PS[:, 4 + gq, 0:S], ACT.Copy))

        ss = sb("ss", [P, 2, NG])
        hn = sb("hn", [P, NG, D])
        sq = sb("sq", [P, NG, D])

        def rmsnorm_rows(x_of, gain, which, after):
            VE.wait(after)
            for k in range(NG):
                m = VE.did(dve.tensor_tensor_reduce(out=sq[:, k, :], in0=x_of(k), in1=x_of(k), scale=1.0, scalar=0.0,
                                                    op0=ALU.mult, op1=ALU.add, accum_out=ss[:, which, k:k + 1]))
            r = rsqrt(ss[:, which, :], ss[:, which, :], NG, 1.0 / D, RMS_EPS, m)
            VE.wait(r)
            for k in range(NG):
                m = VE.did(dve.scalar_tensor_tensor(out=hn[:, k, :], in0=x_of(k), scalar=ss[:, which, k:k + 1],
                                                    in1=gain[:, :], op0=ALU.mult, op1=ALU.mult))
            return m

        def transpose_rows(dst, src_of, bank, after):
            PE.wait(*after)
            for k in range(NG):
                m = pe.transpose(PS[:, bank, k * P:(k + 1) * P], src_of(k), ident[:, :])
            m = PE.did(m)
            AC.wait(m)
            return AC.did(act.activation(dst, PS[:, bank, :], ACT.Copy))

        hn_ready = rmsnorm_rows(lambda k: XS[:, k, 0:D], ln1r, 0, xs_ready)
        hnT = sb("hnT", [P, NG * P])
        hnT_ready = transpose_rows(hnT[:, :], lambda k: hn[:, k, :], 0, (hn_ready,))

        TURN = (6.28125, 0.00193500518798828125, 3.0199159819560e-07)
        MAGIC = 1.5 * 2.0 ** 23
        PI = 3.1415925
        ang = sb("ang", [P, NG, FD // 2])
        turns = sb("turns", [P, NG, FD // 2])
        trig = sb("trig", [P, 2, NG, FD // 2])
        VE.wait(xs_ready, consts)
        m = VE.did(dve.tensor_tensor(ang[:, :, :], XS[:, :, D + 1:D + 2].to_broadcast([P, NG, FD // 2]),
                                     inv_freq[:, :].rearrange("p (o n) -> p o n", o=1).to_broadcast([P, NG, FD // 2]),
                                     ALU.mult))
        VE.wait(m)
        m = VE.did(dve.tensor_scalar(turns[:, :, :], ang[:, :, :], float(1 / (2 * np.pi)), MAGIC, ALU.mult, ALU.add))
        VE.wait(m)
        m = VE.did(dve.tensor_scalar(turns[:, :, :], turns[:, :, :], -MAGIC, None, ALU.add))
        for part in TURN:
            VE.wait(m)
            m = VE.did(dve.scalar_tensor_tensor(out=ang[:, :, :], in0=turns[:, :, :], scalar=-part, in1=ang[:, :, :],
                                                op0=ALU.mult, op1=ALU.add))
        VE.wait(m)
        m = VE.did(dve.tensor_scalar(trig[:, 0, :, :], ang[:, :, :], float(np.pi / 2), None, ALU.add))
        VE.wait(m)
        m = VE.did(dve.tensor_scalar(turns[:, :, :], trig[:, 0, :, :], PI, -2 * np.pi, ALU.is_gt, ALU.mult))
        VE.wait(m)
        m = VE.did(dve.tensor_tensor(trig[:, 0, :, :], trig[:, 0, :, :], turns[:, :, :], ALU.add))
        VE.wait(m)
        VE.did(dve.tensor_scalar(trig[:, 0, :, :], trig[:, 0, :, :], -PI, PI, ALU.max, ALU.min))
        m = VE.did(dve.tensor_scalar(trig[:, 1, :, :], ang[:, :, :], -PI, PI, ALU.max, ALU.min))
        AC.wait(m)
        trig_ready = AC.did(act.activation(trig[:, :, :, :], trig[:, :, :, :], ACT.Sin))

        mrT = sb("mrT", [P, NG, T, P])
        PE.wait(mrow_ready)
        for gq in range(NG):
            for t in range(T):
                m = pe.transpose(PS[:, 4 + gq // 2, ((gq % 2) * T + t) * P:((gq % 2) * T + t + 1) * P],
                                 mrow[:, gq, t:S:T], ident[:, :])
        m = PE.did(m)
        VE.wait(m)
        m = VE.did(dve.tensor_copy(mrT[:, :, :, :],
                                   PS[:, 4:6, :].rearrange("p k (g t q) -> p (k g) t q", t=T, q=P)))
        PE.wait(m)
        for gq in range(NG):
            for b4 in range(4):
                r = slice(32 * b4, 32 * b4 + 32)
                for t in range(T):
                    m = pe.matmul(PS[r, 6, gq * CAP:(gq + 1) * CAP], mrT[:, gq, t, 32 * b4:32 * b4 + 32],
                                  GT[:, (4 * gq + b4) * T + t, :], start=(t == 0), stop=(t == T - 1))
        m = PE.did(m)
        msel = sb("msel", [P, NG, CAP])
        VE.wait(m)
        msel_ready = VE.did(dve.tensor_copy(msel[:, :, :], PS[:, 6, 0:NG * CAP].rearrange("p (g k) -> p g k", k=CAP)))

        QK = sb("QK", [P, NG, 2, FH, 2, FD // 2])
        PE.wait(hnT_ready, fw_in, xs_ready)
        for gq in range(NG):
            m = pe.matmul(PS[:, 1 + gq // 2, (gq % 2) * S:(gq % 2 + 1) * S], hnT[:, gq * P:(gq + 1) * P],
                          fwq[:, :, :], start=True, stop=True)
        m = PE.did(m)
        AC.wait(m)
        qk_ready = AC.did(act.activation(QK[:, :, :, :, :, :].rearrange("p g w h u f -> p (g w h u f)"),
                                         PS[:, 1:3, :].rearrange("p k n -> p (k n)"), ACT.Copy))
        VX = sb("VX", [P, B, FH // 4, 32])
        vbank = (3, 4, 5, 7)
        hn4 = sb("hn4", [P, B, 4, 32])
        AC.wait(hnT_ready)
        m = AC.did(act.activation(
            hn4[:, :, :, :],
            hnT[:, :].rearrange("p (b o k) -> p b o k", o=1, k=32).to_broadcast([P, B, 4, 32]), ACT.Copy))
        PE.wait(msel_ready, m)
        for gq in range(NG):
            for b4 in range(4):
                b = 4 * gq + b4
                m = pe.matmul(PS[:, vbank[gq], b4 * P:(b4 + 1) * P],
                              hn4[:, b, :, :].rearrange("p r k -> p (r k)"),
                              fwv[:, :], start=True, stop=True)
            m = PE.did(m)
            VE.wait(m)
            vx_ready = VE.did(dve.tensor_tensor(
                VX[:, 4 * gq:4 * gq + 4, :, :].rearrange("p b h n -> p (b h) n"),
                PS[:, vbank[gq], :].rearrange("p (b n) -> p b n", n=32),
                blockmask[:, :].rearrange("p (o n) -> p o n", o=1).to_broadcast([P, FH, 32]), ALU.mult))

        QR = sb("QR", [P, NG, 2, FH, 2, FD // 2])
        rt = sb("rt", [P, 2, NG, 2 * FH, FD // 2])
        VE.wait(qk_ready, trig_ready)
        PO.wait(qk_ready, trig_ready)
        for gq in range(NG):
            src = QK[:, gq, :, :, :, :].rearrange("p w h u f -> p (w h) u f")
            dst = QR[:, gq, :, :, :, :].rearrange("p w h u f -> p (w h) u f")
            co, si = (trig[:, k, gq:gq + 1, :].to_broadcast([P, 2 * FH, FD // 2]) for k in range(2))
            VE.did(dve.tensor_tensor(dst[:, :, 0, :], src[:, :, 0, :], co, ALU.mult))
            VE.did(dve.tensor_tensor(dst[:, :, 1, :], src[:, :, 1, :], co, ALU.mult))
            VE.did(dve.tensor_tensor(rt[:, 0, gq, :, :], src[:, :, 1, :], si, ALU.mult))
            m = VE.did(dve.tensor_tensor(rt[:, 1, gq, :, :], src[:, :, 0, :], si, ALU.mult))
        VE.wait(m)
        for gq in range(NG):
            dst = QR[:, gq, :, :, :, :].rearrange("p w h u f -> p (w h) u f")
            VE.did(dve.tensor_tensor(dst[:, :, 0, :], dst[:, :, 0, :], rt[:, 0, gq, :, :], ALU.subtract))
            m = VE.did(dve.tensor_tensor(dst[:, :, 1, :], dst[:, :, 1, :], rt[:, 1, gq, :, :], ALU.add))
        rope_ready = m
        fqT = sb("fqT", [P, NG * P])
        fkT = sb("fkT", [P, NG * P])
        flat = lambda w: (lambda k: QR[:, k, w, :, :, :].rearrange("p h u f -> p (h u f)"))
        fkT_ready = transpose_rows(fkT[:, :], flat(1), 0, (rope_ready, hnT_ready))
        fqT_ready = transpose_rows(fqT[:, :], flat(0), 6, (rope_ready, msel_ready))

        KX = sb("KX", [P, 4, FH, CAP])
        SC = sb("SC", [P, NG, FH, CAP])
        zeroed = PO.did(pool.memset(SC[:, :, :, NSEL:CAP], 0.0))
        fmx = sb("fmx", [P, NG, FH])
        fden = sb("fden", [P, NG, FH])
        sbank = (1, 2, 3, 4)
        kx_used = {}
        PE.wait(fqT_ready, vx_ready, qk_ready)
        for gq in range(NG):
            for b4 in range(4):
                b = 4 * gq + b4
                VE.wait(fkT_ready, kx_used.get(b - 4))
                m = VE.did(dve.tensor_tensor(
                    KX[:, b4, :, :],
                    fkT[:, b * 32:(b + 1) * 32].rearrange("p (o k) -> p o k", o=1).to_broadcast([P, FH, CAP]),
                    headmask[:, :].rearrange("p (h o) -> p h o", o=1).to_broadcast([P, FH, CAP]), ALU.mult))
                PE.wait(m)
                m = PE.did(pe.matmul(PS[32 * b4:32 * b4 + 32, sbank[gq], :], fqT[:, b * 32:(b + 1) * 32],
                                     KX[:, b4, :, :], start=True, stop=True))
                kx_used[b] = m
            VE.wait(m, msel_ready)
            m = VE.did(dve.scalar_tensor_tensor(
                out=SC[:, gq, :, 0:NSEL],
                in0=PS[:, sbank[gq], :].rearrange("p (h k) -> p h k", k=CAP)[:, :, 0:NSEL], scalar=float(FD) ** -0.5,
                in1=msel[:, gq:gq + 1, 0:NSEL].to_broadcast([P, FH, NSEL]), op0=ALU.mult, op1=ALU.add))
            VE.wait(m)
            m = VE.did(dve.tensor_reduce(fmx[:, gq, :], SC[:, gq, :, 0:NSEL], AX_X, ALU.max))
            VE.wait(m)
            m = VE.did(dve.tensor_tensor(
                SC[:, gq, :, 0:NSEL], SC[:, gq, :, 0:NSEL],
                fmx[:, gq, :].rearrange("p (h o) -> p h o", o=1).to_broadcast([P, FH, NSEL]), ALU.subtract))
            AC.wait(m)
            e_done = AC.did(act.activation(SC[:, gq, :, 0:NSEL], SC[:, gq, :, 0:NSEL], ACT.Exp))
            VE.wait(e_done)
            m = VE.did(dve.tensor_reduce(fden[:, gq, :], SC[:, gq, :, 0:NSEL], AX_X, ALU.add))
            VE.wait(m)
            den_ready = VE.did(dve.reciprocal(fden[:, gq, :], fden[:, gq, :]))
        eT = sb("eT", [P, NG, FH // 4, P])
        tbank = (0, 5, 6, 7)
        ON = sb("ON", [P, NG, FH, FD])
        PE.wait(e_done, fkT_ready, fqT_ready, vx_ready, zeroed)
        for gq in range(NG):
            for hh in range(FH // 4):
                m = pe.transpose(PS[:, tbank[gq], hh * P:(hh + 1) * P],
                                 SC[:, gq, 4 * hh:4 * hh + 4, :].rearrange("p h k -> p (h k)"), ident[:, :])
            m = PE.did(m)
            AC.wait(m)
            et_ready = AC.did(act.activation(eT[:, gq, :, :], PS[:, tbank[gq], :].rearrange("p (h q) -> p h q", q=P),
                                             ACT.Copy))
            PE.wait(et_ready, den_ready)
            for b4 in range(4):
                for hh in range(FH // 4):
                    m = pe.matmul(PS[32 * b4:32 * b4 + 32, 1, gq * P + hh * 32:gq * P + hh * 32 + 32],
                                  eT[:, gq, hh, 32 * b4:32 * b4 + 32], VX[:, 4 * gq + b4, hh, :],
                                  start=True, stop=True)
            o_done = PE.did(m)
        VE.wait(o_done)
        m = VE.did(dve.tensor_tensor(
            ON[:, :, :, :].rearrange("p g h d -> p (g h) d"), PS[:, 1, :].rearrange("p (n d) -> p n d", d=FD),
            fden[:, :, :].rearrange("p g (h o) -> p (g h) o", o=1).to_broadcast([P, NG * FH, FD]), ALU.mult))
        oT = sb("oT", [P, NG * P])
        oT_ready = transpose_rows(oT[:, :], lambda k: ON[:, k, :, :].rearrange("p h d -> p (h d)"), 2, (m,))
        PE.wait(oT_ready)
        for gq in range(NG):
            m = pe.matmul(PS[:, 3, gq * P:(gq + 1) * P], oT[:, gq * P:(gq + 1) * P], fwo[:, :], start=True, stop=True)
        m = PE.did(m)
        XA = sb("XA", [P, NG, D])
        VE.wait(m)
        m = VE.did(dve.tensor_tensor(XA[:, :, :], PS[:, 3, :].rearrange("p (g d) -> p g d", d=D), XS[:, :, 0:D],
                                     ALU.add))
        hn2_ready = rmsnorm_rows(lambda k: XA[:, k, :], ln2r, 1, m)
        hn2T = sb("hn2T", [P, NG * P])
        hn2T_ready = transpose_rows(hn2T[:, :], lambda k: hn[:, k, :], 4, (hn2_ready,))

        GS = sb("GS", [P, NG, T, P])
        GTt = sb("GTt", [P, T, B * CAP])
        PO.wait(sel_steps[B - 1])
        for t in range(T):
            gtt = PO.did(pool.tensor_copy(GTt[:, t, :].rearrange("p (b k) -> p b k", k=CAP),
                                          GT[:, :, :].rearrange("p (b t) k -> p t b k", t=T)[:, t, :, :]))
        PE.wait(m, oT_ready, gtt)
        for gq in range(NG):
            for t in range(T):
                src = GTt[:, t, gq * P:(gq + 1) * P]
                m = pe.transpose(PS[:, 2 + gq // 2, ((gq % 2) * T + t) * P:((gq % 2) * T + t + 1) * P], src,
                                 ident[:, :])
        m = PE.did(m)
        VE.wait(m)
        gs_ready = VE.did(dve.tensor_copy(GS[:, :, :, :].rearrange("p g t n -> p (g t n)"),
                                          PS[:, 2:4, :].rearrange("p k n -> p (k n)")))

        HT = sb("HT", [P, F // P, NG * P])
        PE.wait(hn2T_ready, et_ready)
        for f in range(F // P):
            m = PE.did(pe.matmul(PS[:, tbank[f], :], fw1[:, f * P:(f + 1) * P], hn2T[:, :], start=True, stop=True))
            AC.wait(m)
            ht_ready = AC.did(act.activation(HT[:, f, :], PS[:, tbank[f], :], ACT.Gelu_apprx_tanh))
        PE.wait(ht_ready)
        for gq in range(NG):
            for f in range(F // P):
                m = pe.matmul(PS[:, 1, gq * P:(gq + 1) * P], HT[:, f, gq * P:(gq + 1) * P], fw2[:, f, :],
                              start=(f == 0), stop=(f == F // P - 1))
        m = PE.did(m)
        VE.wait(m)
        m = VE.did(dve.tensor_tensor(XA[:, :, :], PS[:, 1, :].rearrange("p (g d) -> p g d", d=D), XA[:, :, :], ALU.add))
        VE.wait(m)
        for gq in range(NG):
            m = VE.did(dve.tensor_scalar(XA[:, gq, :], XA[:, gq, :], XS[:, gq, D:D + 1], None, ALU.mult))

        PE.wait(m, gs_ready, ht_ready, hn2T_ready)
        out_dram = out.rearrange("b (p t) d -> p b t d", t=T)
        stored = Arrival(sem("stored"))
        for g2 in range(2):
            for gl in range(2):
                for t in range(T):
                    for b4 in range(4):
                        gq = 2 * g2 + gl
                        r = slice(32 * b4, 32 * b4 + 32)
                        mm = pe.matmul(PS[:, 2 * b4 + g2, (gl * T + t) * P:(gl * T + t + 1) * P], GS[r, gq, t, :],
                                       XA[r, gq, :], start=True, stop=True)
            m = PE.did(mm)
            VE.wait(m)
            for b4 in range(4):
                xv = X[:, :, :].rearrange("p (g b t) d -> p g b t d", b=4, t=T)[:, 2 * g2:2 * g2 + 2, b4, :, :]
                m = VE.did(dve.tensor_tensor(xv, PS[:, 2 * b4 + g2, :].rearrange("p (g t d) -> p g t d", g=2, t=T), xv,
                                             ALU.add))
            SP.wait(m)
            last = stored.of(sp.dma_start(out_dram[:, 8 * g2:8 * g2 + 8, :, :], X4[:, 8 * g2:8 * g2 + 8, :, :]))
        SP.wait(last)


_NAMES = {
    "x": "x", "ctx_768": "ctx_768", "w_v": "L0_attn_w_v", "b_q": "L0_attn_b_q", "b_k": "L0_attn_b_k",
    "b_v": "L0_attn_b_v", "b_out": "L0_attn_b_out", "xWo": "L0_xattn_Wo", "xbo": "L0_xattn_bo",
    "attention_mask": "L0_ffn_attention_mask", "position_ids": "L0_ffn_position_ids",
    "router_w": "L0_ffn_router_w", "router_b": "L0_ffn_router_b", "fwq": "L0_ffn_wq", "fwk": "L0_ffn_wk",
    "fwv": "L0_ffn_wv", "fwo": "L0_ffn_wo", "fw1": "L0_ffn_w1", "fw2": "L0_ffn_w2", "ln1": "L0_ffn_ln1",
    "ln2": "L0_ffn_ln2",
}
_TRANSPOSED = {
    "w_qT": "L0_attn_w_q", "w_kT": "L0_attn_w_k", "w_outT": "L0_attn_w_out", "xWqT": "L0_xattn_Wq",
    "xWkT": "L0_xattn_Wk", "xWvT": "L0_xattn_Wv",
}


def kernel(**inputs):
    import concourse.bacc as bacc
    from concourse.bass_utils import run_bass_kernel_spmd

    nc = bacc.Bacc("TRN2", target_bir_lowering=False, num_devices=1)
    arrays, aps = {}, {}
    for names, flip in ((_NAMES, False), (_TRANSPOSED, True)):
        for name, source in names.items():
            v = np.asarray(inputs[source])
            v = np.ascontiguousarray(v.T if flip else v)
            arrays[f"in_{name}"] = v
            aps[name] = nc.dram_tensor(f"in_{name}", v.shape, mybir.dt.from_np(v.dtype), kind="ExternalInput").ap()
    out = nc.dram_tensor("out_x", (B, S, D), F32, kind="ExternalOutput").ap()
    build(nc, aps, out)
    r = run_bass_kernel_spmd(nc, [arrays], core_ids=[0])
    return r.results[0]["out_x"]
```

```python
from contextlib import ExitStack

import numpy as np

import concourse.bass as bass
from concourse import mybir

F32 = mybir.dt.float32
BF16 = mybir.dt.bfloat16
I32 = mybir.dt.int32
ALU = mybir.AluOpType
ACT = mybir.ActivationFunctionType
AX_X = mybir.AxisListType.X

P = 128
B, S, D = 16, 256, 128
T = S // P
NC, DC = 1601, 96
H, DH = 16, 64
KT = 13
KP = -(-NC // KT)
KFULL = NC - (KP - 1) * KT
HP = H // 2
W2 = 2 * S
TILES = HP * KT
F = 512
FH, FD = 16, 8
CAP = S // 8
NSEL = CAP - 1
MB, MS = 4, 512
NG = B // 4
LN_EPS, RMS_EPS = 1e-5, 1e-6
ROPE_BASE = 10000.0
PRING = 8
AV_LAG = 4


class Mark:

    def __init__(self, sem, value):
        self.sem, self.value = sem, value


class Engine:

    def __init__(self, eng, sem):
        self.eng, self.sem, self.n, self.seen = eng, sem, 0, {}

    def did(self, ins):
        self.n += 1
        ins.then_inc(self.sem, 1)
        return Mark(self.sem, self.n)

    def wait(self, *marks):
        for m in marks:
            if m is not None and self.seen.get(id(m.sem), 0) < m.value:
                self.eng.wait_ge(m.sem, m.value)
                self.seen[id(m.sem)] = m.value


class Arrival:

    def __init__(self, sem):
        self.sem, self.n = sem, 0

    def of(self, dma):
        self.n += 16
        dma.then_inc(self.sem, 16)
        return Mark(self.sem, self.n)


def build(nc, a, out):
    with ExitStack() as ctx:

        def sb(name, shape, dt=F32, until=ctx):
            return until.enter_context(nc.sbuf_tensor(name, shape, dt))

        def sem(name):
            return ctx.enter_context(nc.semaphore(name))

        PE = Engine(nc.tensor, sem("pe_steps"))
        AC = Engine(nc.scalar, sem("act_steps"))
        VE = Engine(nc.vector, sem("dve_steps"))
        PO = Engine(nc.gpsimd, sem("pool_steps"))
        SP = Engine(nc.sync, sem("sp_steps"))
        pe, act, dve, pool, sp = PE.eng, AC.eng, VE.eng, PO.eng, SP.eng
        arrival = {}

        def load(key, dst, src):
            if key not in arrival:
                arrival[key] = Arrival(sem("in_" + key))
            return arrival[key].of(sp.dma_start(dst, src))

        PS = ctx.enter_context(nc.psum_tensor("PS", [P, 8, 512], F32))

        ident = sb("ident", [P, P])
        identb = sb("identb", [P, P], BF16)
        minus_half = sb("minus_half", [P, 8])
        lower = sb("lower", [P, T, T, P], BF16)
        slots = sb("slots", [P, CAP])
        sloti = sb("sloti", [P, CAP], I32)
        headmask = sb("headmask", [P, FH])
        blockmask = sb("blockmask", [P, 32])
        inv_freq = sb("inv_freq", [P, FD // 2])

        wqT = sb("wqT", [P, P])
        wkT = sb("wkT", [P, P])
        wvo = sb("wvo", [P, P])
        cols = sb("cols", [P, 3])
        xbo = sb("xbo", [P, P])
        crow = sb("crow", [P, P])
        fwq = sb("fwq", [P, 2, P])
        fwv = sb("fwv", [P, P])
        fwo = sb("fwo", [P, P])
        fw1 = sb("fw1", [P, F])
        fw2 = sb("fw2", [P, F // P, P])
        ln1r = sb("ln1r", [P, P])
        ln2r = sb("ln2r", [P, P])
        rwr = sb("rwr", [P, P])
        rbc = sb("rbc", [P, 1])
        posi = sb("posi", [P, MB, T], I32)
        msk = sb("msk", [P, MB, T, S])

        X = sb("X", [P, B * T, D])
        XW = D + 1 + FD
        X3 = sb("X3", [P, 4, T, XW])
        GT = sb("GT", [P, 4, T, CAP])

        stats = sb("stats", [P, 3, T, 6])
        mv = sb("mv", [P, 3, T, 2])
        rstd = sb("rstd", [P, 3, T])
        junk = sb("junk", [P, 8, S], BF16)
        cnt = sb("cnt", [P, 2, 3, T])
        wraw = sb("wraw", [P, 2, T])
        keep = sb("keep", [P, 2, T])
        rank = sb("rank", [P, 2, T])
        posf = sb("posf", [P, MB * T])
        ang = sb("ang", [P, MB * T, FD // 2])
        turns = sb("turns", [P, MB * T, FD // 2])
        trig = sb("trig", [P, MB, T, 2, FD // 2])
        XS = sb("XS", [P, XW])
        mrow = sb("mrow", [P, S])
        mrT = sb("mrT", [P, T, P])
        msel = sb("msel", [P, CAP])
        ss = sb("ss", [P, 2])
        hn = sb("hn", [P, D])
        sq = sb("sq", [P, D])
        hnT = sb("hnT", [P, P])
        hn4 = sb("hn4", [P, 4, 4, 32])
        QK = sb("QK", [P, 2, FH, 2, FD // 2])
        QR = sb("QR", [P, 2, FH, 2, FD // 2])
        rt = sb("rt", [P, 2, 2 * FH, FD // 2])
        fqkT = sb("fqkT", [P, 2, P])
        VX = sb("VX", [P, 4, FH // 4, 32])
        KX = sb("KX", [P, 4, FH, CAP])
        SC = sb("SC", [P, FH, CAP])
        fmx = sb("fmx", [P, FH])
        fden = sb("fden", [P, FH])
        eT = sb("eT", [P, FH // 4, P])
        ON = sb("ON", [P, FH, FD])
        oT = sb("oT", [P, P])
        XA = sb("XA", [P, D])
        hn2T = sb("hn2T", [P, P])
        GTt = sb("GTt", [P, T, 4 * CAP])
        GS = sb("GS", [P, T, P])
        HT = sb("HT", [P, F // P, P])

        X2T = sb("X2T", [P, 2, 4, S], BF16)
        G = sb("G", [P, 2, H, DC], BF16)
        M = sb("M", [DC + 1, H, D + 1])
        rxa = sb("rxa", [P, 2, T])
        Cf = sb("Cf", [KP, KT, DC])
        Ch = [sb(f"Ch{i}", [KP, KT, DC + 1], BF16) for i in range(2)]
        Cl = [sb(f"Cl{i}", [KP, KT, DC], BF16) for i in range(2)]
        ChT = [sb(f"ChT{i}", [DC + 2, KT, KP], BF16) for i in range(2)]
        ClT = [sb(f"ClT{i}", [DC, KT, KP], BF16) for i in range(2)]
        AH = [sb(f"AH{i}", [DC + 2, H * S], BF16) for i in range(2)]
        AL = [sb(f"AL{i}", [DC, H * S], BF16) for i in range(2)]
        U = [sb(f"U{i}", [DC + 1, W2]) for i in range(2)]
        pmax = sb("pmax", [P, 2, H * T, 2])
        nmax = sb("nmax", [P, 2, H * T])
        mh = sb("mh", [H * T, P], BF16)
        ml = sb("ml", [H * T, P], BF16)

        xn = sb("xn", [P, T, D])
        xT = sb("xT", [P, S])
        qT = sb("qT", [P, S])
        kT = sb("kT", [P, S])
        vp = sb("vp", [P, T, D])
        nm = sb("nm", [P, T])
        den = sb("den", [P, T])
        rden = sb("rden", [P, T])
        ex = sb("ex", [P, T, S])
        exT = sb("exT", [P, T, T, P])
        xn2 = sb("xn2", [P, T, D])
        raw = ctx.enter_context(ExitStack())
        wv, woutT, brow = (sb(n, [P, P], until=raw) for n in ("wv", "woutT", "brow"))
        big = {n: sb(n, [P, HP, D if n in ("xWqT", "xWo") else DC], until=raw)
               for n in ("xWqT", "xWkT", "xWvT", "xWo")}

        def load_context(b):
            c = a["ctx_768"]
            last = (KP - 1) * KT
            SP.wait(c_split.get(b - 1))
            load("ctx", Cf[0:KP - 1, :, :], c[b, 0:last, :].rearrange("(p t) d -> p t d", t=KT))
            load("ctx", Cf[KP - 1:KP, 0:KFULL, :],
                 c[b, last:NC, :].rearrange("(o t) d -> o t d", o=1))
            return load("ctx", Cf[KP - 1:KP, KFULL:KT, :],
                        c[b, NC - (KT - KFULL):NC, :].rearrange("(o t) d -> o t d", o=1))

        c_split = {}
        x_dram = a["x"].rearrange("b (p t) d -> p b t d", t=T)
        X4 = X[:, :, :].rearrange("p (b t) d -> p b t d", t=T)

        def load_x(b):
            return load(f"x{b}", X4[:, b, :, :], x_dram[:, b, :, :])

        def row(name):
            return a[name].rearrange("(o n) -> o n", o=1).to_broadcast([P, a[name].shape[0]])

        x_in = [load_x(0)]
        for n, t in (("w_qT", wqT), ("w_kT", wkT)):
            load("wqk", t[:, :], a[n])
        for i, n in enumerate(("b_q", "b_k", "b_v")):
            wqk_in = load("wqk", cols[:, i:i + 1], a[n].rearrange("(p o) -> p o", o=1))
        ctx_in = {0: load_context(0)}
        for n, t in (("w_v", wv), ("w_outT", woutT)):
            load("wvo", t[:, :], a[n])
        load("wvo", brow[:, :], row("b_out"))
        wvo_in = load("wvo", xbo[:, :], row("xbo"))
        big_in = {}
        for q in range(2):
            js = slice(4 * q, 4 * q + 4)
            for n in big:
                big_in[q] = load(f"xw{q}", big[n][:, js, :], a[n].rearrange("(j p) n -> p j n", p=P)[:, js, :])
            if q == 0:
                x_in.append(load_x(1))
        for n, t in (("ln1", ln1r), ("ln2", ln2r)):
            load("rows", t[:, :], row(n))
        load("rows", rwr[:, :], a["router_w"].rearrange("n o -> o n").to_broadcast([P, P]))
        rows_in = load("rows", rbc[:, :], row("router_b"))
        pos_in = load("pos", posi[:, :, :], a["position_ids"][:, 0:S].rearrange("b (p t) -> p b t", t=T))

        def load_rest():
            x_in.extend(load_x(b) for b in range(2, B))
            for n, t in (("wq", fwq[:, 0, :]), ("wk", fwq[:, 1, :]), ("wv", fwv[:, :]), ("wo", fwo[:, :]),
                         ("w1", fw1[:, :]), ("w2", fw2[:, :, :])):
                src = a["f" + n]
                load("fw", t, src.rearrange("(j p) n -> p j n", p=P) if n == "w2" else src)
            for mb in range(MB):
                m = load("fw", msk[:, mb, :, :],
                         a["attention_mask"][mb, 0, 0:S, 0:S].rearrange("(p t) n -> p t n", t=T))
            return m

        def const(ins):
            m = PO.did(ins)
            PO.wait(m)
            return m

        for t in (ident, identb):
            const(pool.memset(t[:, :], 0.0))
            ident_ready = const(pool.affine_select(out=t[:, :], in_=t[:, :], compare_op=ALU.not_equal, fill=1.0,
                                                   base=0, pattern=[[-1, P]], channel_multiplier=1))
        const(pool.memset(minus_half[:, :], -0.5))

        def other_constants():
            const(pool.memset(lower[:, :, :, :], 1.0))
            const(pool.memset(headmask[:, :], 1.0))
            const(pool.memset(blockmask[:, :], 1.0))
            for i in range(FD // 2):
                inv = float(np.float32(1.0) / np.power(np.float32(ROPE_BASE), np.float32(2 * i / FD)))
                const(pool.memset(inv_freq[:, i:i + 1], inv))
            for t in range(T):
                const(pool.affine_select(out=lower[:, t, :, :], in_=lower[:, t, :, :], compare_op=ALU.is_gt, fill=0.0,
                                          base=t, pattern=[[-1, T], [-T, P]], channel_multiplier=T))
            const(pool.affine_select(out=headmask[:, :], in_=headmask[:, :], compare_op=ALU.is_ge, fill=0.0,
                                           base=0, pattern=[[-FD, FH]], channel_multiplier=1))
            const(pool.affine_select(out=blockmask[:, :].rearrange("p (h d) -> p h d", d=FD),
                                           in_=blockmask[:, :].rearrange("p (h d) -> p h d", d=FD),
                                           compare_op=ALU.is_ge, fill=0.0,
                                           base=0, pattern=[[-32, 4], [0, FD]], channel_multiplier=1))
            const(pool.affine_select(out=headmask[:, :], in_=headmask[:, :], compare_op=ALU.is_ge, fill=0.0,
                                      base=FD - 1, pattern=[[FD, FH]], channel_multiplier=-1))
            const(pool.affine_select(out=blockmask[:, :].rearrange("p (h d) -> p h d", d=FD),
                                      in_=blockmask[:, :].rearrange("p (h d) -> p h d", d=FD),
                                      compare_op=ALU.is_ge, fill=0.0,
                                      base=31, pattern=[[32, 4], [0, FD]], channel_multiplier=-1))
            const(pool.iota(sloti[:, :], pattern=[[1, CAP]], base=0, channel_multiplier=0))
            const(pool.tensor_copy(slots[:, :], sloti[:, :]))
            const(pool.memset(slots[:, NSEL:CAP], -1.0))
            for i in range(2):
                const(pool.memset(ChT[i][DC:DC + 2, :, :], 1.0))
                const(pool.memset(Ch[i][:, :, DC:DC + 1], 1.0))
            const(pool.memset(SC[:, :, NSEL:CAP], 0.0))
            const(pool.memset(M[:, :, :], 0.0))
            return const(pool.memset(M[DC:DC + 1, :, D:D + 1], 1.0))

        def rsqrt(dst, var, n, scale, eps, after):
            PO.wait(after)
            m = PO.did(pool.tensor_scalar(dst, var, scale, eps, ALU.mult, ALU.add))
            PO.wait(m)
            return PO.did(pool.tensor_tensor(dst, dst, minus_half[:, 0:n], ALU.pow))

        def make_wvo():
            PE.wait(wqk_in, wvo_in, small_free[0])
            pe.matmul(PS[:, 7, 0:P], wv[:, :], woutT[:, :], start=True, stop=True)
            m = PE.did(pe.matmul(PS[:, 7, P:2 * P], cols[:, 2:3].to_broadcast([P, P]), woutT[:, :],
                                 start=True, stop=True))
            VE.wait(m, wvo_in)
            VE.did(dve.tensor_copy(wvo[:, :], PS[:, 7, 0:P]))
            small_free[0] = m = VE.did(dve.tensor_tensor(crow[:, :], PS[:, 7, P:2 * P], brow[:, :], ALU.add))
            return m

        def make_G_M(q):
            banks = ((2, 3, 4, 5), (0, 1, 6, 4))[q]
            G2 = G[:, :, :, :].rearrange("p w (j e) c -> p w e j c", e=2)
            M2 = M[:, :, :].rearrange("p (j e) c -> p e j c", e=2)
            js = slice(4 * q, 4 * q + 4)
            heads = [(j, j % 4 * P) for j in range(4 * q, 4 * q + 4)]

            def make_g(even):
                rows, bank = slice(DH * even, DH * even + DH), banks[even]
                PE.wait(big_in[q])
                for j, c in heads:
                    m = pe.matmul(PS[:, bank, c:c + DC], big["xWqT"][rows, j, :], big["xWkT"][rows, j, :],
                                  start=True, stop=True)
                m = PE.did(m)
                g = PS[:, bank, :].rearrange("p (h c) -> p h c", c=P)[:, :, 0:DC]
                AC.wait(m)
                hi = AC.did(act.activation(G2[:, 0, even, js, :], g, ACT.Copy, scale=DH ** -0.5))
                VE.wait(hi)
                gm_read[bank] = VE.did(dve.scalar_tensor_tensor(
                    out=G2[:, 1, even, js, :], in0=g, scalar=DH ** -0.5, in1=G2[:, 0, even, js, :],
                    op0=ALU.mult, op1=ALU.subtract))

            def make_m(even):
                rows, bank = slice(DH * even, DH * even + DH), banks[2 + even]
                PE.wait(big_in[q], gm_read.get(bank))
                for j, c in heads:
                    m = pe.matmul(PS[0:DC, bank, c:c + D], big["xWvT"][rows, j, :], big["xWo"][rows, j, :],
                                  start=True, stop=True)
                m = PE.did(m)
                VE.wait(m, consts)
                gm_ready[q] = gm_read[bank] = VE.did(dve.tensor_copy(
                    M2[0:DC, even, js, 0:D], PS[0:DC, bank, :].rearrange("p (h c) -> p h c", c=P)))

            return [lambda: make_g(0), lambda: make_g(1), lambda: make_m(0), lambda: make_m(1)]

        gm_ready, gm_read = {}, {}

        ln_last = {}

        def norm_stats(which, b, x_mark):
            VE.wait(x_mark, ln_last.get(which))
            for t in range(T):
                m = VE.did(dve.bn_stats(stats[:, which, t, :], X[:, T * b + t, :]))
            VE.wait(m)
            for t in range(T):
                m = VE.did(dve.bn_aggr(mv[:, which, t, :], stats[:, which, t, :]))
            ln_last["rstd", which] = rsqrt(rstd[:, which, :], mv[:, which, :, 1], T, 1.0, LN_EPS, m)

        def norm_apply(which, b, dst_of, dst_free=None):
            VE.wait(ln_last["rstd", which], dst_free)
            for t in range(T):
                m = VE.did(dve.tensor_scalar(dst_of(t), X[:, T * b + t, :], mv[:, which, t, 0:1],
                                             rstd[:, which, t:t + 1], ALU.subtract, ALU.mult))
            ln_last[which] = m
            return m

        small_free = [None]
        SA_SCALE = float(D) ** -0.5
        sa = {}
        bo_added, x2T_ready = {}, {}

        def sa_transpose(b):
            PE.wait(sa["xn"], ident_ready, small_free[0])
            for t in range(T):
                m = pe.transpose(PS[:, 7, t * P:(t + 1) * P], xn[:, t, :], ident[:, :])
            sa["xn_read"] = PE.did(m)
            AC.wait(sa["xn_read"], sa.get("xT_read"))
            small_free[0] = sa["xT"] = AC.did(act.activation(xT[:, :], PS[:, 7, 0:S], ACT.Copy))

        def sa_query_key(b):
            PE.wait(sa["xT"], wqk_in, small_free[0])
            pe.matmul(PS[:, 7, 0:S], wqT[:, :], xT[:, :], start=True, stop=True)
            m = PE.did(pe.matmul(PS[:, 7, S:2 * S], wkT[:, :], xT[:, :], start=True, stop=True))
            VE.wait(m, sa.get("scores"))
            q = VE.did(dve.tensor_scalar(qT[:, :], PS[:, 7, 0:S], cols[:, 0:1], SA_SCALE, ALU.add, ALU.mult))
            AC.wait(m, q, sa.get("scores"))
            small_free[0] = sa["qk"] = AC.did(act.activation(kT[:, :], PS[:, 7, S:2 * S], ACT.Identity,
                                                             bias=cols[:, 1:2]))

        def sa_value(b):
            PE.wait(wvo_ready, small_free[0])
            for t in range(T):
                m = pe.matmul(PS[:, 7, t * P:(t + 1) * P], xT[:, t * P:(t + 1) * P], wvo[:, :], start=True, stop=True)
            sa["xT_read"] = PE.did(m)
            AC.wait(sa["xT_read"], sa.get("out"))
            small_free[0] = sa["v"] = AC.did(act.activation(vp[:, :, :], PS[:, 7, 0:T * D].rearrange(
                "p (t d) -> p t d", d=D), ACT.Copy))

        def sa_scores(b):
            PE.wait(sa["qk"], small_free[0])
            for t in range(T):
                m = pe.matmul(PS[:, 7, t * S:(t + 1) * S], qT[:, t * P:(t + 1) * P], kT[:, :], start=True, stop=True)
            sa["scores"] = PE.did(m)
            VE.wait(sa["scores"], sa.get("ex"))
            m = VE.did(dve.tensor_reduce(nm[:, :], PS[:, 7, :].rearrange("p (t n) -> p t n", n=S), AX_X, ALU.max,
                                         negate=True))
            AC.wait(m, sa.get("ex_read"), sa.get("x1"))
            for t in range(T):
                m = AC.did(act.activation(ex[:, t, :], PS[:, 7, t * S:(t + 1) * S], ACT.Exp,
                                          bias=nm[:, t:t + 1], accum_out=den[:, t:t + 1]))
            small_free[0] = sa["ex"] = m

        def sa_turn(b):
            PE.wait(sa["ex"], small_free[0])
            for kt in range(T):
                for t in range(T):
                    c = (kt * T + t) * P
                    m = pe.transpose(PS[:, 7, c:c + P], ex[:, t, kt * P:(kt + 1) * P], ident[:, :])
            sa["ex_read"] = PE.did(m)
            AC.wait(sa["ex_read"], sa.get("out"))
            small_free[0] = sa["exT"] = AC.did(act.activation(
                exT[:, :, :, :], PS[:, 7, :].rearrange("p (k t q) -> p k t q", k=T, t=T), ACT.Copy))
            PO.wait(sa["xn"], wvo_ready)
            for t in range(T):
                m = PO.did(pool.tensor_tensor(X[:, T * b + t, :], X[:, T * b + t, :], crow[:, :], ALU.add))
            sa["x+c"] = m

        def sa_output(b):
            PE.wait(sa["exT"], sa["v"], small_free[0])
            for t in range(T):
                for kt in range(T):
                    m = pe.matmul(PS[:, 7, t * P:(t + 1) * P], exT[:, kt, t, :], vp[:, kt, :],
                                  start=(kt == 0), stop=(kt == T - 1))
            sa["out"] = PE.did(m)
            VE.wait(sa["ex"])
            r = VE.did(dve.reciprocal(rden[:, :], den[:, :]))
            VE.wait(sa["out"], sa["x+c"], r)
            for t in range(T):
                m = VE.did(dve.scalar_tensor_tensor(out=X[:, T * b + t, :], in0=PS[:, 7, t * P:(t + 1) * P],
                                                    scalar=rden[:, t:t + 1], in1=X[:, T * b + t, :],
                                                    op0=ALU.mult, op1=ALU.add))
            small_free[0] = sa["x1"] = m

        def sa_norm2(b):
            sa["xn2"] = m = norm_apply(1, b, lambda t: xn2[:, t, :], sa.get("xn2_read"))
            PO.wait(m, wvo_in)
            for t in range(T):
                bo_added[b] = PO.did(pool.tensor_tensor(X[:, T * b + t, :], X[:, T * b + t, :], xbo[:, :], ALU.add))

        def sa_finish(b):
            PE.wait(sa["xn2"], small_free[0])
            for t in range(T):
                m = pe.transpose(PS[:, 7, t * P:(t + 1) * P], xn2[:, t, :], ident[:, :])
            sa["xn2_read"] = PE.did(m)
            AC.wait(sa["xn2_read"])
            m = AC.did(act.activation(X2T[:, 0, b % 4, :], PS[:, 7, 0:S], ACT.Copy))
            VE.wait(m)
            small_free[0] = x2T_ready[b] = VE.did(dve.tensor_tensor(X2T[:, 1, b % 4, :], PS[:, 7, 0:S], X2T[:, 0, b % 4, :],
                                                                    ALU.subtract))

        def self_attention(b):
            def first_norm():
                sa["xn"] = norm_apply(0, b, lambda t: xn[:, t, :], sa.get("xn_read"))

            return [lambda: norm_stats(0, b, x_in[b]), first_norm] + [
                lambda f=f: f(b) for f in (sa_transpose, sa_query_key, sa_value, sa_scores, sa_turn, sa_output)
            ] + [lambda: norm_stats(1, b, sa["x1"]), lambda: sa_norm2(b), lambda: sa_finish(b)]

        raw.close()
        PF = sb("PF", [KP, PRING, W2])
        PL = sb("PL", [KP, PRING, W2], BF16)
        PH = PF[:, :, :].bitcast(BF16).rearrange("p r (n w) -> p r n w", w=2)[:, :, :, 1]
        MAXB = {0: 0, 1: 2}
        NQ = 4
        NKEY = KT * KP // NQ
        max_free, st_free, acc_free = {}, {}, [None]
        av_done, exp_done, lo_done = {}, {}, {}
        u_free = {0: None, 1: None}
        st_used, av_used = {}, {}
        x_added = {}

        def split_context(b):
            i = b % 2
            if b < 2:
                AC.wait(ctx_in[b])
                VE.wait(AC.did(act.activation(Ch[i][:, :, 0:DC], Cf[:, :, :], ACT.Copy)))
                c_split[b] = VE.did(dve.tensor_tensor(Cl[i][:, :, :], Cf[:, :, :], Ch[i][:, :, 0:DC], ALU.subtract))
                return
            PO.wait(ctx_in[b], av_used.get(b - 2), c_tr.get(b - 2))
            m = PO.did(pool.tensor_copy(Ch[i][:, :, 0:DC], Cf[:, :, :]))
            PO.wait(m)
            c_split[b] = PO.did(pool.tensor_tensor(Cl[i][:, :, :], Cf[:, :, :], Ch[i][:, :, 0:DC], ALU.subtract))

        c_tr, c_ready = {}, {}

        def transpose_context(b, part, t0, t1):
            i = b % 2
            src, dst = (Ch, ChT) if part == 0 else (Cl, ClT)
            bank = PS[0:DC, 7, :].bitcast(BF16)
            PE.wait(c_split[b], small_free[0], ident_ready)
            for t in range(t0, t1):
                m = pe.transpose(bank[:, (t - t0) * KP:(t - t0 + 1) * KP], src[i][:, t, 0:DC], identb[0:KP, 0:KP])
            c_tr[b] = PE.did(m)
            AC.wait(c_tr[b], st_used.get(b - 2))
            m = AC.did(act.activation(dst[i][0:DC, t0:t1, :],
                                      bank[:, 0:(t1 - t0) * KP].rearrange("p (t k) -> p t k", k=KP), ACT.Copy))
            small_free[0] = c_ready[b] = m

        a_ready = {}

        def make_queries(b, hp):
            i = b % 2
            PE.wait(x2T_ready[b], small_free[0], gm_ready[hp // 4])
            for j in range(2):
                for n, (w, x) in enumerate(((0, 0), (0, 1), (1, 0))):
                    m = pe.matmul(PS[0:DC, 7, j * S:(j + 1) * S], G[:, w, 2 * hp + j, :], X2T[:, x, b % 4, :],
                                  start=(n == 0), stop=(n == 2))
            m = PE.did(m)
            cols_ = slice(hp * W2, (hp + 1) * W2)
            AC.wait(m, st_used.get(b - 2))
            hi = AC.did(act.activation(AH[i][0:DC, cols_], PS[0:DC, 7, :], ACT.Copy))
            VE.wait(hi)
            m = VE.did(dve.tensor_tensor(AL[i][:, cols_], PS[0:DC, 7, :], AH[i][0:DC, cols_], ALU.subtract))
            small_free[0] = a_ready[(b, hp)] = m

        def max_chunk(b, ht, half):
            i, k = b % 2, (2 * ht + half) % 2
            PE.wait(c_ready[b], a_ready[(b, ht // 4)], max_free[k])
            keys = ChT[i][0:DC, :, :].rearrange("p t k -> p (t k)")
            for n in range(2):
                c = (2 * half + n) * NKEY
                m = pe.matmul(PS[:, MAXB[k] + n, 0:NKEY], AH[i][0:DC, ht * P:(ht + 1) * P], keys[:, c:c + NKEY],
                              start=True, stop=True)
            m = PE.did(m)
            VE.wait(m)
            m = VE.did(dve.tensor_reduce(pmax[:, i, ht, half:half + 1], PS[:, MAXB[k]:MAXB[k] + 2, 0:NKEY],
                                         mybir.AxisListType.XY, ALU.max))
            max_free[k] = m
            pmax_done[b] = m

        m_in, m_last, nmax_done, pmax_done = {}, [None], {}, {}

        def reduce_max(b, h0, h1):
            i = b % 2
            VE.wait(pmax_done[b])
            nmax_done[b] = VE.did(dve.tensor_reduce(nmax[:, i, T * h0:T * h1], pmax[:, i, T * h0:T * h1, :], AX_X,
                                                    ALU.max, negate=True))

        def place_max(b, h0, h1):
            i, n = b % 2, T * (h1 - h0)
            PE.wait(nmax_done[b], small_free[0])
            m = PE.did(pe.transpose(PS[0:n, 7, 0:P], nmax[:, i, T * h0:T * h1], ident[:, :]))
            AC.wait(m, m_last[0])
            hi = AC.did(act.activation(mh[0:n, :], PS[0:n, 7, 0:P], ACT.Copy))
            VE.wait(hi, m_last[0])
            lo = VE.did(dve.tensor_tensor(ml[0:n, :], PS[0:n, 7, 0:P], mh[0:n, :], ALU.subtract))
            small_free[0] = lo
            SP.wait(hi, lo, st_used.get(b - 2))
            load("negmax", AH[i][DC:DC + 1, h0 * S:h1 * S], mh[0:n, :])
            m_last[0] = load("negmax", AH[i][DC + 1:DC + 2, h0 * S:h1 * S], ml[0:n, :])
            for hp in range(h0 // 2, h1 // 2):
                m_in[b, hp] = m_last[0]

        def scores_tile(n):
            b, hp, t = n // TILES, n % TILES // KT, n % KT
            i, k, r = b % 2, n % 2, n % PRING
            cols_ = slice(hp * W2, (hp + 1) * W2)
            PE.wait(m_in[b, hp], a_ready[(b, hp)], c_ready[b], st_free[k], consts)
            o = PS[0:KP, 4 + k, :]
            pe.matmul(o, ChT[i][:, t, :], AH[i][:, cols_], start=True, stop=False)
            pe.matmul(o, ChT[i][0:DC, t, :], AL[i][:, cols_], start=False, stop=False)
            m = PE.did(pe.matmul(o, ClT[i][:, t, :], AH[i][0:DC, cols_], start=False, stop=True))
            st_used[b] = m
            AC.wait(m, av_done.get(n - PRING))
            exp_done[n] = st_free[k] = AC.did(act.activation(PF[:, r, :], o, ACT.Exp))
            if n % 2:
                VE.wait(exp_done[n], av_done.get(n - PRING))
                lo_done[n] = lo_done[n - 1] = VE.did(dve.tensor_tensor(
                    PL[:, r - 1:r + 1, :], PF[:, r - 1:r + 1, :], PH[:, r - 1:r + 1, :], ALU.subtract))

        def values_tile(n):
            b, hp, t = n // TILES, n % TILES // KT, n % KT
            i, r = b % 2, n % PRING
            rows = KP if t < KFULL else KP - 1
            PE.wait(exp_done[n], c_split[b], consts)
            if t == 0:
                PE.wait(acc_free[0])
            c_hi, c_lo = Ch[i][0:rows, t, :], Cl[i][0:rows, t, :]
            pe.matmul(PS[0:DC + 1, 6, :], c_hi, PH[0:rows, r, :], start=(t == 0), stop=False)
            pe.matmul(PS[0:DC, 6, :], c_lo, PH[0:rows, r, :], start=False, stop=False)
            PE.wait(lo_done[n])
            m = PE.did(pe.matmul(PS[0:DC + 1, 6, :], c_hi, PL[0:rows, r, :], start=False, stop=(t == KT - 1)))
            av_done[n] = av_used[b] = m
            if t == KT - 1:
                k = (b * HP + hp) % 2
                AC.wait(m, u_free[k])
                acc_free[0] = u_ready[(b, hp)] = AC.did(act.activation(U[k][:, :], PS[0:DC + 1, 6, :], ACT.Copy))

        u_ready, x2_ready = {}, {}

        def project_head(b, h):
            k = (b * HP + h // 2) % 2
            PE.wait(u_ready[(b, h // 2)], small_free[0], gm_ready[h // 8])
            for t in range(T):
                c = (h % 2) * S + t * P
                m = pe.matmul(PS[:, 7, t * (D + 1):(t + 1) * (D + 1)], U[k][:, c:c + P], M[:, h, :],
                              start=True, stop=True)
            m = PE.did(m)
            u_free[k] = m
            o = PS[:, 7, 0:T * (D + 1)].rearrange("p (t n) -> p t n", n=D + 1)
            VE.wait(m, x_added.get(h % 2))
            m = VE.did(dve.reciprocal(rxa[:, h % 2, :], o[:, :, D]))
            VE.wait(m, x_added.get("x"), bo_added[b])
            for t in range(T):
                m = VE.did(dve.scalar_tensor_tensor(out=X[:, T * b + t, :], in0=o[:, t, 0:D],
                                                    scalar=rxa[:, h % 2, t:t + 1], in1=X[:, T * b + t, :],
                                                    op0=ALU.mult, op1=ALU.add))
            small_free[0] = x_added["x"] = x_added[h % 2] = x2_ready[b] = m

        sel_steps = {}
        ring_read = {}

        TURN = (6.28125, 0.00193500518798828125, 3.0199159819560e-07)
        MAGIC = 1.5 * 2.0 ** 23
        PI = 3.1415925
        trig_ready = [None]

        def make_trig():
            n, f = MB * T, FD // 2
            VE.wait(pos_in, consts)
            m = VE.did(dve.tensor_copy(posf[:, :], posi[:, :, :].rearrange("p b t -> p (b t)")))
            VE.wait(m)
            m = VE.did(dve.tensor_tensor(ang[:, :, :], posf[:, :].rearrange("p (n o) -> p n o", o=1)
                                         .to_broadcast([P, n, f]),
                                         inv_freq[:, :].rearrange("p (o f) -> p o f", o=1).to_broadcast([P, n, f]),
                                         ALU.mult))
            VE.wait(m)
            m = VE.did(dve.tensor_scalar(turns[:, :, :], ang[:, :, :], float(1 / (2 * np.pi)), MAGIC, ALU.mult,
                                         ALU.add))
            VE.wait(m)
            m = VE.did(dve.tensor_scalar(turns[:, :, :], turns[:, :, :], -MAGIC, None, ALU.add))
            for part in TURN:
                VE.wait(m)
                m = VE.did(dve.scalar_tensor_tensor(out=ang[:, :, :], in0=turns[:, :, :], scalar=-part,
                                                    in1=ang[:, :, :], op0=ALU.mult, op1=ALU.add))
            tr = trig[:, :, :, :, :].rearrange("p b t w f -> p (b t) w f")
            VE.wait(m)
            m = VE.did(dve.tensor_scalar(tr[:, :, 0, :], ang[:, :, :], float(np.pi / 2), None, ALU.add))
            VE.wait(m)
            m = VE.did(dve.tensor_scalar(turns[:, :, :], tr[:, :, 0, :], PI, -2 * np.pi, ALU.is_gt, ALU.mult))
            VE.wait(m)
            m = VE.did(dve.tensor_tensor(tr[:, :, 0, :], tr[:, :, 0, :], turns[:, :, :], ALU.add))
            VE.wait(m)
            VE.did(dve.tensor_scalar(tr[:, :, 0, :], tr[:, :, 0, :], -PI, PI, ALU.max, ALU.min))
            m = VE.did(dve.tensor_scalar(tr[:, :, 1, :], ang[:, :, :], -PI, PI, ALU.max, ALU.min))
            AC.wait(m)
            trig_ready[0] = AC.did(act.activation(trig[:, :, :, :, :], trig[:, :, :, :, :], ACT.Sin))

        def select_weights(b):
            i = b % 4
            m = norm_apply(2, b, lambda t: X3[:, i, t, 0:D], ring_read.get("X3"))
            VE.wait(m, rows_in, trig_ready[0])
            for t in range(T):
                m = VE.did(dve.tensor_tensor_reduce(out=junk[:, 6 + t, 0:D], in0=X3[:, i, t, 0:D], in1=rwr[:, :],
                                                    scale=1.0, scalar=0.0, op0=ALU.mult, op1=ALU.add,
                                                    accum_out=wraw[:, b % 2, t:t + 1]))
            VE.wait(m)
            VE.did(dve.tensor_copy(X3[:, i, :, D + 1:XW], trig[:, min(b, MB - 1), :, :, :].rearrange(
                "p t w f -> p t (w f)")))
            sel_steps["w"] = VE.did(dve.tensor_scalar(X3[:, i, :, D], wraw[:, b % 2, :], rbc[:, 0:1], None,
                                                      ALU.add))

        def select_row(b):
            PE.wait(sel_steps["w"], small_free[0])
            for t in range(T):
                m = pe.transpose(PS[:, 7, t * P:(t + 1) * P], X3[:, b % 4, t, D:D + 1].to_broadcast([P, P]),
                                 ident[:, :])
            sel_steps["row"] = PE.did(m)

        def select_rank(b):
            i = b % 2
            row = PS[:, 7, 0:S]
            VE.wait(sel_steps["row"], consts)
            for t in range(T):
                w = X3[:, b % 4, t, D:D + 1]
                for j, op in enumerate((ALU.is_gt, ALU.is_ge)):
                    VE.did(dve.tensor_scalar(junk[:, 2 * t + j, :], row, w, None, op, ALU.add,
                                             accum_out=cnt[:, i, j, t:t + 1]))
                m = VE.did(dve.scalar_tensor_tensor(out=junk[:, 4 + t, :], in0=row, scalar=w,
                                                    in1=lower[:, t, :, :].rearrange("p u q -> p (u q)"),
                                                    op0=ALU.is_equal, op1=ALU.mult, accum_out=cnt[:, i, 2, t:t + 1]))
            small_free[0] = m
            VE.wait(m)
            VE.did(dve.tensor_tensor(rank[:, i, :], cnt[:, i, 0, :], cnt[:, i, 2, :], ALU.add))
            m = VE.did(dve.tensor_scalar(keep[:, i, :], cnt[:, i, 1, :], NSEL + 0.5, None, ALU.is_gt))
            VE.wait(m, ring_read.get("GT"), ring_read.get("GTt"))
            for t in range(T):
                VE.did(dve.tensor_scalar(GT[:, b % 4, t, :], slots[:, :], rank[:, i, t:t + 1], None, ALU.is_equal))
                m = VE.did(dve.scalar_tensor_tensor(out=X[:, T * b + t, :], in0=X3[:, b % 4, t, 0:D],
                                                    scalar=keep[:, i, t:t + 1], in1=X[:, T * b + t, :],
                                                    op0=ALU.mult, op1=ALU.add))
            sel_steps[b] = m

        out_dram = out.rearrange("b (p t) d -> p b t d", t=T)
        stored, stored_last = Arrival(sem("stored")), [None]
        wide = {"free": {}, "next": 0}

        def chosen(gq, last):
            done = {}

            def bank():
                if not last:
                    PE.wait(small_free[0])
                    return 7
                k = wide["next"] % 8
                wide["next"] += 1
                if k not in wide["free"]:
                    PE.wait(small_free[0], acc_free[0], max_free[0], max_free[1], st_free[0], st_free[1])
                PE.wait(wide["free"].get(k))
                return k

            def free(k, mark):
                if last:
                    wide["free"][k] = mark
                else:
                    small_free[0] = mark

            rows = [slice(32 * b4, 32 * b4 + 32) for b4 in range(4)]

            def gather_rows():
                PE.wait(sel_steps[4 * gq + 3], fw_in)
                k = bank()
                for b4 in range(4):
                    for t in range(T):
                        pe.matmul(PS[rows[b4], k, 0:XW], GT[:, b4, t, :], X3[:, b4, t, :],
                                  start=(t == 0), stop=(t == T - 1))
                    for t in range(T):
                        m = pe.matmul(PS[rows[b4], k, S:2 * S], GT[:, b4, t, :],
                                      msk[:, min(4 * gq + b4, MB - 1), t, :], start=(t == 0), stop=(t == T - 1))
                ring_read["X3"] = m = PE.did(m)
                VE.wait(m)
                done["xs"] = VE.did(dve.tensor_copy(XS[:, :], PS[:, k, 0:XW]))
                AC.wait(m, done["xs"])
                done["mrow"] = AC.did(act.activation(mrow[:, :], PS[:, k, S:2 * S], ACT.Copy))
                free(k, done["mrow"])
                PO.wait(sel_steps[4 * gq + 3])
                for t in range(T):
                    ring_read["GTt"] = done["gtt"] = PO.did(pool.tensor_copy(GTt[:, t, :].rearrange("p (b k) -> p b k", k=CAP),
                                                          GT[:, :, t, :]))

            def rms_stats(x, which, after):
                VE.wait(done[after])
                m = VE.did(dve.tensor_tensor_reduce(out=sq[:, :], in0=x, in1=x, scale=1.0, scalar=0.0, op0=ALU.mult,
                                                    op1=ALU.add, accum_out=ss[:, which:which + 1]))
                done["rms", which] = rsqrt(ss[:, which:which + 1], ss[:, which:which + 1], 1, 1.0 / D, RMS_EPS, m)

            def rms_apply(x, gain, which):
                VE.wait(done["rms", which], rows_in)
                done["hn", which] = VE.did(dve.scalar_tensor_tensor(out=hn[:, :], in0=x, scalar=ss[:, which:which + 1],
                                                                    in1=gain[:, :], op0=ALU.mult, op1=ALU.mult))

            def turn_rows():
                k = bank()
                PE.wait(done["hn", 0], done["mrow"])
                pe.transpose(PS[:, k, 0:P], hn[:, :], ident[:, :])
                for t in range(T):
                    m = pe.transpose(PS[:, k, (1 + t) * P:(2 + t) * P], mrow[:, t:S:T], ident[:, :])
                m = PE.did(m)
                AC.wait(m)
                done["hnT"] = AC.did(act.activation(hnT[:, :], PS[:, k, 0:P], ACT.Copy))
                VE.wait(m, done["hnT"])
                done["mrT"] = VE.did(dve.tensor_copy(mrT[:, :, :], PS[:, k, P:(1 + T) * P].rearrange(
                    "p (t q) -> p t q", q=P)))
                free(k, done["mrT"])
                PO.wait(done["hnT"])
                done["hn4"] = PO.did(pool.tensor_copy(
                    hn4[:, :, :, :],
                    hnT[:, :].rearrange("p (b o k) -> p b o k", o=1, k=32).to_broadcast([P, 4, 4, 32])))

            def query_key_mask():
                k = bank()
                PE.wait(done["mrT"], fw_in)
                for b4 in range(4):
                    for t in range(T):
                        pe.matmul(PS[rows[b4], k, 0:CAP], mrT[:, t, rows[b4]], GT[:, b4, t, :],
                                  start=(t == 0), stop=(t == T - 1))
                ring_read["GT"] = m = PE.did(pe.matmul(PS[:, k, S:2 * S], hnT[:, :], fwq[:, :, :], start=True, stop=True))
                VE.wait(m)
                done["msel"] = VE.did(dve.tensor_copy(msel[:, :], PS[:, k, 0:CAP]))
                AC.wait(m, done["msel"])
                done["qk"] = AC.did(act.activation(QK[:, :, :, :, :].rearrange("p w h u f -> p (w h u f)"),
                                                   PS[:, k, S:2 * S], ACT.Copy))
                free(k, done["qk"])

            def rope():
                VE.wait(done["qk"])
                src = QK[:, :, :, :, :].rearrange("p w h u f -> p (w h) u f")
                dst = QR[:, :, :, :, :].rearrange("p w h u f -> p (w h) u f")
                c0 = D + 1
                co, si = (XS[:, c0 + w * FD // 2:c0 + (w + 1) * FD // 2].rearrange("p (o f) -> p o f", o=1)
                          .to_broadcast([P, 2 * FH, FD // 2]) for w in range(2))
                VE.did(dve.tensor_tensor(dst[:, :, 0, :], src[:, :, 0, :], co, ALU.mult))
                VE.did(dve.tensor_tensor(dst[:, :, 1, :], src[:, :, 1, :], co, ALU.mult))
                VE.did(dve.tensor_tensor(rt[:, 0, :, :], src[:, :, 1, :], si, ALU.mult))
                m = VE.did(dve.tensor_tensor(rt[:, 1, :, :], src[:, :, 0, :], si, ALU.mult))
                VE.wait(m)
                VE.did(dve.tensor_tensor(dst[:, :, 0, :], dst[:, :, 0, :], rt[:, 0, :, :], ALU.subtract))
                done["rope"] = VE.did(dve.tensor_tensor(dst[:, :, 1, :], dst[:, :, 1, :], rt[:, 1, :, :], ALU.add))

            def values():
                k = bank()
                PE.wait(done["hn4"])
                for b4 in range(4):
                    m = pe.matmul(PS[:, k, b4 * P:(b4 + 1) * P], hn4[:, b4, :, :].rearrange("p r k -> p (r k)"),
                                  fwv[:, :], start=True, stop=True)
                m = PE.did(m)
                VE.wait(m)
                done["vx"] = VE.did(dve.tensor_tensor(
                    VX[:, :, :, :].rearrange("p b h n -> p (b h) n"),
                    PS[:, k, :].rearrange("p (b n) -> p b n", n=32),
                    blockmask[:, :].rearrange("p (o n) -> p o n", o=1).to_broadcast([P, FH, 32]), ALU.mult))
                free(k, done["vx"])

            def turn_query_key():
                k = bank()
                PE.wait(done["rope"])
                for w in range(2):
                    m = pe.transpose(PS[:, k, w * P:(w + 1) * P],
                                     QR[:, w, :, :, :].rearrange("p h u f -> p (h u f)"), ident[:, :])
                m = PE.did(m)
                AC.wait(m)
                done["fqkT"] = AC.did(act.activation(fqkT[:, :, :], PS[:, k, 0:2 * P].rearrange("p (w q) -> p w q", q=P),
                                                     ACT.Copy))
                free(k, done["fqkT"])

            def spread_keys():
                for e, half in ((VE, (0, 1)), (PO, (2, 3))):
                    e.wait(done["fqkT"])
                    for b4 in half:
                        m = e.did(e.eng.tensor_tensor(
                            KX[:, b4, :, :],
                            fqkT[:, 1, rows[b4]].rearrange("p (o k) -> p o k", o=1).to_broadcast([P, FH, CAP]),
                            headmask[:, :].rearrange("p (h o) -> p h o", o=1).to_broadcast([P, FH, CAP]), ALU.mult))
                    done["kx", half[0]] = m

            def scores():
                k = bank()
                PE.wait(done["kx", 0], done["kx", 2])
                for b4 in range(4):
                    m = pe.matmul(PS[rows[b4], k, :], fqkT[:, 0, rows[b4]], KX[:, b4, :, :], start=True, stop=True)
                m = PE.did(m)
                VE.wait(m, consts)
                m = VE.did(dve.scalar_tensor_tensor(
                    out=SC[:, :, 0:NSEL], in0=PS[:, k, :].rearrange("p (h k) -> p h k", k=CAP)[:, :, 0:NSEL],
                    scalar=float(FD) ** -0.5,
                    in1=msel[:, 0:NSEL].rearrange("p (o k) -> p o k", o=1).to_broadcast([P, FH, NSEL]),
                    op0=ALU.mult, op1=ALU.add))
                free(k, m)
                VE.wait(m)
                m = VE.did(dve.tensor_reduce(fmx[:, :], SC[:, :, 0:NSEL], AX_X, ALU.max))
                VE.wait(m)
                m = VE.did(dve.tensor_tensor(
                    SC[:, :, 0:NSEL], SC[:, :, 0:NSEL],
                    fmx[:, :].rearrange("p (h o) -> p h o", o=1).to_broadcast([P, FH, NSEL]), ALU.subtract))
                AC.wait(m)
                done["exp"] = AC.did(act.activation(SC[:, :, 0:NSEL], SC[:, :, 0:NSEL], ACT.Exp))

            def denominators():
                VE.wait(done["exp"])
                m = VE.did(dve.tensor_reduce(fden[:, :], SC[:, :, 0:NSEL], AX_X, ALU.add))
                VE.wait(m)
                done["den"] = VE.did(dve.reciprocal(fden[:, :], fden[:, :]))

            def turn_exp():
                k = bank()
                PE.wait(done["exp"])
                for hh in range(FH // 4):
                    m = pe.transpose(PS[:, k, hh * P:(hh + 1) * P],
                                     SC[:, 4 * hh:4 * hh + 4, :].rearrange("p h k -> p (h k)"), ident[:, :])
                m = PE.did(m)
                AC.wait(m)
                done["eT"] = AC.did(act.activation(eT[:, :, :], PS[:, k, :].rearrange("p (h q) -> p h q", q=P), ACT.Copy))
                free(k, done["eT"])

            def attend():
                k = bank()
                PE.wait(done["eT"], done["vx"])
                for b4 in range(4):
                    for hh in range(FH // 4):
                        m = pe.matmul(PS[rows[b4], k, hh * 32:hh * 32 + 32], eT[:, hh, rows[b4]], VX[:, b4, hh, :],
                                      start=True, stop=True)
                m = PE.did(m)
                VE.wait(m, done["den"])
                done["on"] = VE.did(dve.tensor_tensor(
                    ON[:, :, :], PS[:, k, 0:P].rearrange("p (n d) -> p n d", d=FD),
                    fden[:, :].rearrange("p (h o) -> p h o", o=1).to_broadcast([P, FH, FD]), ALU.mult))
                free(k, done["on"])

            def turn_attended():
                k = bank()
                PE.wait(done["on"])
                m = PE.did(pe.transpose(PS[:, k, 0:P], ON[:, :, :].rearrange("p h d -> p (h d)"), ident[:, :]))
                AC.wait(m)
                done["oT"] = AC.did(act.activation(oT[:, :], PS[:, k, 0:P], ACT.Copy))
                free(k, done["oT"])

            def project_out():
                k = bank()
                PE.wait(done["oT"])
                m = PE.did(pe.matmul(PS[:, k, 0:D], oT[:, :], fwo[:, :], start=True, stop=True))
                VE.wait(m)
                done["xa"] = VE.did(dve.tensor_tensor(XA[:, :], PS[:, k, 0:D], XS[:, 0:D], ALU.add))
                free(k, done["xa"])

            def turn_hidden():
                k = bank()
                PE.wait(done["hn", 1], done["gtt"])
                for t in range(T):
                    pe.transpose(PS[:, k, (1 + t) * P:(2 + t) * P], GTt[:, t, :], ident[:, :])
                m = PE.did(pe.transpose(PS[:, k, 0:P], hn[:, :], ident[:, :]))
                AC.wait(m)
                done["hn2T"] = AC.did(act.activation(hn2T[:, :], PS[:, k, 0:P], ACT.Copy))
                VE.wait(m, done["hn2T"])
                done["gs"] = VE.did(dve.tensor_copy(GS[:, :, :], PS[:, k, P:(1 + T) * P].rearrange(
                    "p (t q) -> p t q", q=P)))
                free(k, done["gs"])

            def mlp_up():
                k = bank()
                PE.wait(done["hn2T"])
                for f in range(F // P):
                    m = pe.matmul(PS[:, k, f * P:(f + 1) * P], fw1[:, f * P:(f + 1) * P], hn2T[:, :],
                                  start=True, stop=True)
                m = PE.did(m)
                AC.wait(m)
                done["ht"] = AC.did(act.activation(HT[:, :, :], PS[:, k, :].rearrange("p (f n) -> p f n", n=P),
                                                   ACT.Gelu_apprx_tanh))
                free(k, done["ht"])

            def mlp_down():
                k = bank()
                PE.wait(done["ht"])
                for f in range(F // P):
                    m = pe.matmul(PS[:, k, 0:D], HT[:, f, :], fw2[:, f, :], start=(f == 0), stop=(f == F // P - 1))
                m = PE.did(m)
                VE.wait(m)
                m = VE.did(dve.tensor_tensor(XA[:, :], PS[:, k, 0:D], XA[:, :], ALU.add))
                free(k, m)
                VE.wait(m)
                done["proc"] = VE.did(dve.tensor_scalar(XA[:, :], XA[:, :], XS[:, D:D + 1], None, ALU.mult))

            def scatter(b4):
                b = 4 * gq + b4
                k = bank()
                PE.wait(done["proc"], done["gs"])
                for t in range(T):
                    m = pe.matmul(PS[:, k, t * D:(t + 1) * D], GS[rows[b4], t, :], XA[rows[b4], :],
                                  start=True, stop=True)
                m = PE.did(m)
                VE.wait(m)
                m = VE.did(dve.tensor_tensor(X[:, T * b:T * b + T, :], PS[:, k, 0:T * D].rearrange(
                    "p (t d) -> p t d", d=D), X[:, T * b:T * b + T, :], ALU.add))
                free(k, m)
                SP.wait(m)
                stored_last[0] = stored.of(sp.dma_start(out_dram[:, b, :, :], X4[:, b, :, :]))

            return [(True, gather_rows), (False, lambda: rms_stats(XS[:, 0:D], 0, "xs")),
                    (False, lambda: rms_apply(XS[:, 0:D], ln1r, 0)), (True, turn_rows), (True, query_key_mask),
                    (False, rope), (True, values), (True, turn_query_key), (False, spread_keys), (True, scores),
                    (True, turn_exp), (False, denominators), (True, attend), (True, turn_attended),
                    (True, project_out), (False, lambda: rms_stats(XA[:, :], 1, "xa")),
                    (False, lambda: rms_apply(XA[:, :], ln2r, 1)), (True, turn_hidden), (True, mlp_up),
                    (True, mlp_down)] + [(True, lambda b4=b4: scatter(b4)) for b4 in range(4)]

        def chosen_plan():
            at = {}
            for gq in range(NG - 1):
                places = iter([TILES * b + k for b in range(4 * gq + 4, 4 * gq + 8) for k in PLACES[20:28]])
                n = 0
                for uses_bank, step in chosen(gq, False):
                    n = next(p for p in places if p > n) if uses_bank else n + 1
                    at.setdefault(n // TILES, []).append((n % TILES, step))
            return at

        def maxima(b, h0, h1):
            return [lambda ht=ht, half=half: max_chunk(b, ht, half) for ht in range(T * h0, T * h1)
                    for half in range(2)] + [lambda: reduce_max(b, h0, h1), lambda: place_max(b, h0, h1)]

        def transposes_of(b):
            return [lambda t0=t0, part=part: transpose_context(b, part, t0, min(t0 + 7, KT))
                    for part in range(2) for t0 in (0, 7)]

        def queries_of(b, first, last):
            return [lambda hp=hp: make_queries(b, hp) for hp in range(first, last)]

        def spread(steps, first, last):
            return [(first + k * (last - first + 1) // len(steps), step) for k, step in enumerate(steps)]

        def chunks(b, h0, h1):
            return maxima(b, h0, h1)[:-2]

        PLACES = [k for k in range(AV_LAG + 6, TILES) if (k - AV_LAG) % KT in (6, 8, 10, 12)]
        LAST = TILES - 4

        def plan(b):
            p, n = PLACES, b + 1
            todo = []
            if b >= 1:
                after = AV_LAG + 5
                todo += [(after, lambda: norm_stats(2, b - 1, x2_ready[b - 1])),
                         (after + 2, lambda: select_weights(b - 1)), (p[4], lambda: select_row(b - 1)),
                         (p[4] + 1, lambda: select_rank(b - 1))]
            if n < B and b >= 1:
                tr, qu = transposes_of(n), queries_of(n, 0, HP)
                places = (p[0], p[1], p[5], p[6])
                todo += list(zip(places, tr))
                todo += list(zip((p[2], p[3], p[7], p[11], p[15], p[16], p[18], p[19]), qu))
                c = chunks(n, 0, H)
                todo += spread(c[:8], p[2] + 1, p[4] - 1) + spread(c[8:], p[6] + 2, LAST - 4)
                sa_places = (p[8], p[9], p[10], p[12], p[13], p[14], p[17])
            if b == 0:
                todo += list(zip((0, 2, 4, 6, 8, 10), queries_of(0, 2, HP)))
                for q in range(1, 4):
                    h = q * EARLY
                    end = 2 * KT * q - 7 if q == 1 else (p[9], p[12])[q - 2] - 1
                    todo += spread(chunks(0, h, h + EARLY), (2, 20, 37)[q - 1], end - 1)
                    todo += [(end, lambda h=h: reduce_max(0, h, h + EARLY)),
                             (end + 1, lambda h=h: place_max(0, h, h + EARLY))]
                todo += list(zip((p[1], p[2], p[3], p[4]), transposes_of(1)))
                todo += list(zip((p[5], p[6], p[7], p[8], p[10], p[11], p[13], p[14]), queries_of(1, 0, HP)))
                todo += spread(chunks(1, 0, H), 50, LAST - 3)
                sa_places = (p[15], p[16], p[17], p[18], p[19], p[20], p[23])
            if n < B:
                todo += [(LAST - 2, lambda: reduce_max(n, 0, H)), (LAST, lambda: place_max(n, 0, H))]
            if b + 2 < B:
                s = self_attention(b + 2)
                q = sa_places
                tiles = (q[0] - 6, q[0] - 3, *q[:6], q[5] + 2, q[5] + 5, q[6])
                todo += list(zip(tiles, s))
            return sorted(todo + beside_groups.get(b, []), key=lambda x: x[0])

        beside_groups = chosen_plan()

        EARLY = 4
        first = self_attention(0)
        gm = make_G_M(0) + make_G_M(1)
        for step in first[:4]:
            step()
            if step is first[0]:
                consts = other_constants()
        wvo_ready = make_wvo()
        for step in first[4:6]:
            step()
        split_context(0)
        ctx_in[1] = load_context(1)
        fw_in = load_rest()
        for step in first[6:] + transposes_of(0):
            gm.pop(0)() if gm else None
            step()
        max_free.update({0: gm_read[1], 1: gm_read[3]})
        st_free.update({0: gm_read[4], 1: gm_read[5]})
        acc_free[0] = gm_read[6]
        for step in queries_of(0, 0, 2):
            step()
        split_context(1)
        beside = self_attention(1) + [make_trig]
        for k, step in enumerate(chunks(0, 0, EARLY)):
            step()
            if k < len(beside):
                beside[k]()
        reduce_max(0, 0, EARLY)
        place_max(0, 0, EARLY)
        TOTAL = B * TILES
        for n in range(TOTAL + AV_LAG):
            b, k = n // TILES, n % TILES
            if k == 0 and b < B:
                todo = plan(b)
                if 1 <= b and b + 1 < B:
                    ctx_in[b + 1] = load_context(b + 1)
            if k == AV_LAG and 1 <= b and b + 1 < B:
                split_context(b + 1)
            if n < TOTAL:
                scores_tile(n)
            if n >= AV_LAG:
                values_tile(n - AV_LAG)
            while todo and todo[0][0] <= k and b < B:
                todo.pop(0)[1]()
            done = n - AV_LAG - (KT - 1)
            for late, j in ((2, 0), (4, 1)):
                if done >= late and (done - late) % KT == 0:
                    w = (done - late) // KT
                    project_head(w // HP, 2 * (w % HP) + j)
        project_head(B - 1, H - 2)
        project_head(B - 1, H - 1)
        norm_stats(2, B - 1, x2_ready[B - 1])
        select_weights(B - 1)
        select_row(B - 1)
        select_rank(B - 1)

        for _, step in chosen(NG - 1, True):
            step()
        SP.wait(stored_last[0])


_NAMES = {
    "x": "x", "ctx_768": "ctx_768", "w_v": "L0_attn_w_v", "b_q": "L0_attn_b_q", "b_k": "L0_attn_b_k",
    "b_v": "L0_attn_b_v", "b_out": "L0_attn_b_out", "xWo": "L0_xattn_Wo", "xbo": "L0_xattn_bo",
    "attention_mask": "L0_ffn_attention_mask", "position_ids": "L0_ffn_position_ids",
    "router_w": "L0_ffn_router_w", "router_b": "L0_ffn_router_b", "fwq": "L0_ffn_wq", "fwk": "L0_ffn_wk",
    "fwv": "L0_ffn_wv", "fwo": "L0_ffn_wo", "fw1": "L0_ffn_w1", "fw2": "L0_ffn_w2", "ln1": "L0_ffn_ln1",
    "ln2": "L0_ffn_ln2",
}
_TRANSPOSED = {
    "w_qT": "L0_attn_w_q", "w_kT": "L0_attn_w_k", "w_outT": "L0_attn_w_out", "xWqT": "L0_xattn_Wq",
    "xWkT": "L0_xattn_Wk", "xWvT": "L0_xattn_Wv",
}


def kernel(**inputs):
    import concourse.bacc as bacc
    from concourse.bass_utils import run_bass_kernel_spmd

    nc = bacc.Bacc("TRN2", target_bir_lowering=False, num_devices=1)
    arrays, aps = {}, {}
    for names, flip in ((_NAMES, False), (_TRANSPOSED, True)):
        for name, source in names.items():
            v = np.asarray(inputs[source])
            v = np.ascontiguousarray(v.T if flip else v)
            arrays[f"in_{name}"] = v
            aps[name] = nc.dram_tensor(f"in_{name}", v.shape, mybir.dt.from_np(v.dtype), kind="ExternalInput").ap()
    out = nc.dram_tensor("out_x", (B, S, D), F32, kind="ExternalOutput").ap()
    build(nc, aps, out)
    r = run_bass_kernel_spmd(nc, [arrays], core_ids=[0])
    return r.results[0]["out_x"]
```
